# Optimizing a Trainium2 kernel written in Bass

```python
import numpy as np
import jax
import jax.numpy as jnp

def _softmax(x, axis=-1):
    return jax.nn.softmax(x, axis=axis)

def _gelu(x):
    return jax.nn.gelu(x, approximate=True)

def _silu(x):
    return jax.nn.silu(x)

def _sigmoid(x):
    return jax.nn.sigmoid(x)

def _layernorm(x, axis=-1, eps=1e-05):
    m = jnp.mean(x, axis=axis, keepdims=True)
    v = jnp.var(x, axis=axis, keepdims=True)
    return (x - m) / jnp.sqrt(v + eps)

def _scatter_add(tgt, idx, src, axis=0):
    return tgt.at[idx].add(src)

def _segment_sum(src, seg, n):
    return jax.ops.segment_sum(src, seg, n)
kernel_name = 'mk_recurrent_d1_jaxref_r8_381217'

def setup_inputs(seed: int=0):
    np.random.seed(seed)
    _w = jnp.asarray

    def _L0_attn_setup():
        import jax, jax.numpy as jnp
        import numpy as np
        N_HEADS = 16
        HEAD_DIM = 64
        ROPE_THETA = 10000.0

        def _rope_cos_sin(seq_len, dim, theta):
            inv_freq = 1.0 / theta ** (jnp.arange(0, dim, 2, dtype=jnp.float32) / dim)
            pos = jnp.arange(seq_len, dtype=jnp.float32)
            freqs = pos[:, None] * inv_freq[None, :]
            emb = jnp.concatenate([freqs, freqs], axis=-1)
            return (jnp.cos(emb), jnp.sin(emb))

        def _rotate_half(x):
            d = x.shape[-1] // 2
            return jnp.concatenate([-x[..., d:], x[..., :d]], axis=-1)
        key = jax.random.key(seed)
        ks = jax.random.split(key, 6)
        B, S, D_MODEL, LATENT = (1, 512, 128, 64)
        q_dim = N_HEADS * HEAD_DIM
        sd = lambda fan_in: 1.0 / np.sqrt(fan_in)
        return {'x': jax.random.normal(ks[0], (B, S, D_MODEL), jnp.float32), 'wq': jax.random.normal(ks[1], (q_dim, D_MODEL), jnp.float32) * sd(D_MODEL), 'w_kv_down': jax.random.normal(ks[2], (LATENT, D_MODEL), jnp.float32) * sd(D_MODEL), 'w_k_up': jax.random.normal(ks[3], (q_dim, LATENT), jnp.float32) * sd(LATENT), 'w_v_up': jax.random.normal(ks[4], (q_dim, LATENT), jnp.float32) * sd(LATENT), 'wo': jax.random.normal(ks[5], (D_MODEL, q_dim), jnp.float32) * sd(q_dim)}
    _L0_attn_in = _L0_attn_setup()

    def _L0_ffn_setup():
        import jax, jax.numpy as jnp
        import numpy as np
        DIM = 128
        NUM_EXPERTS = 8
        TOP_K = 2
        key = jax.random.key(seed)
        ks = jax.random.split(key, 7)
        s_in = 1.0 / np.sqrt(DIM)
        s_hid = 1.0 / np.sqrt(4 * DIM)
        x = jax.random.normal(ks[0], (2, 256, DIM), dtype=jnp.float32)
        gate_w = jax.random.normal(ks[1], (DIM, NUM_EXPERTS), dtype=jnp.float32) * s_in
        gate_b = jax.random.normal(ks[2], (NUM_EXPERTS,), dtype=jnp.float32) * 0.01
        w1 = jax.random.normal(ks[3], (NUM_EXPERTS, DIM, 4 * DIM), dtype=jnp.float32) * s_in
        b1 = jax.random.normal(ks[4], (NUM_EXPERTS, 4 * DIM), dtype=jnp.float32) * 0.01
        w2 = jax.random.normal(ks[5], (NUM_EXPERTS, 4 * DIM, DIM), dtype=jnp.float32) * s_hid
        b2 = jax.random.normal(ks[6], (NUM_EXPERTS, DIM), dtype=jnp.float32) * 0.01
        return {'x': x, 'gate_w': gate_w, 'gate_b': gate_b, 'w1': w1, 'b1': b1, 'w2': w2, 'b2': b2}
    _L0_ffn_in = _L0_ffn_setup()
    _d = {'L0_attn_x': _L0_attn_in['x'], 'L0_attn_wq': _L0_attn_in['wq'], 'L0_attn_w_kv_down': _L0_attn_in['w_kv_down'], 'L0_attn_w_k_up': _L0_attn_in['w_k_up'], 'L0_attn_w_v_up': _L0_attn_in['w_v_up'], 'L0_attn_wo': _L0_attn_in['wo'], 'L0_ffn_gate_w': _L0_ffn_in['gate_w'], 'L0_ffn_gate_b': _L0_ffn_in['gate_b'], 'L0_ffn_w1': _L0_ffn_in['w1'], 'L0_ffn_b1': _L0_ffn_in['b1'], 'L0_ffn_w2': _L0_ffn_in['w2'], 'L0_ffn_b2': _L0_ffn_in['b2']}
    _x0 = _d['L0_attn_x']
    _d['L0_attn_x'] = jax.random.normal(jax.random.fold_in(jax.random.key(seed), 1), (8, 256, 128), dtype=_x0.dtype)
    del _x0
    return _d

def reference(L0_attn_x, L0_attn_wq, L0_attn_w_kv_down, L0_attn_w_k_up, L0_attn_w_v_up, L0_attn_wo, L0_ffn_gate_w, L0_ffn_gate_b, L0_ffn_w1, L0_ffn_b1, L0_ffn_w2, L0_ffn_b2):

    def _L0_attn_ref(x, wq, w_kv_down, w_k_up, w_v_up, wo):
        import jax, jax.numpy as jnp
        import numpy as np
        N_HEADS = 16
        HEAD_DIM = 64
        ROPE_THETA = 10000.0

        def _rope_cos_sin(seq_len, dim, theta):
            inv_freq = 1.0 / theta ** (jnp.arange(0, dim, 2, dtype=jnp.float32) / dim)
            pos = jnp.arange(seq_len, dtype=jnp.float32)
            freqs = pos[:, None] * inv_freq[None, :]
            emb = jnp.concatenate([freqs, freqs], axis=-1)
            return (jnp.cos(emb), jnp.sin(emb))

        def _rotate_half(x):
            d = x.shape[-1] // 2
            return jnp.concatenate([-x[..., d:], x[..., :d]], axis=-1)
        B, S, _ = x.shape
        H, D = (N_HEADS, HEAD_DIM)
        q = jnp.einsum('bsd,qd->bsq', x, wq).reshape(B, S, H, D).transpose(0, 2, 1, 3)
        kv_latent = jnp.einsum('bsd,ld->bsl', x, w_kv_down)
        k = jnp.einsum('bsl,ql->bsq', kv_latent, w_k_up).reshape(B, S, H, D).transpose(0, 2, 1, 3)
        v = jnp.einsum('bsl,ql->bsq', kv_latent, w_v_up).reshape(B, S, H, D).transpose(0, 2, 1, 3)
        cos, sin = _rope_cos_sin(S, D, ROPE_THETA)
        cos = cos[None, None]
        sin = sin[None, None]
        q = q * cos + _rotate_half(q) * sin
        k = k * cos + _rotate_half(k) * sin
        scores = jnp.einsum('bhsd,bhtd->bhst', q, k) / jnp.sqrt(jnp.float32(D))
        causal = jnp.triu(jnp.full((S, S), -jnp.inf, dtype=jnp.float32), k=1)
        scores = scores + causal[None, None]
        probs = jax.nn.softmax(scores.astype(jnp.float32), axis=-1).astype(q.dtype)
        out = jnp.einsum('bhst,bhtd->bhsd', probs, v)
        out = out.transpose(0, 2, 1, 3).reshape(B, S, H * D)
        return jnp.einsum('bsq,dq->bsd', out, wo)

    def _L0_ffn_ref(x, gate_w, gate_b, w1, b1, w2, b2):
        import jax, jax.numpy as jnp
        import numpy as np
        DIM = 128
        NUM_EXPERTS = 8
        TOP_K = 2
        B, N, C = x.shape
        flat_x = x.reshape(-1, C)
        logits = flat_x @ gate_w + gate_b
        _, topk_idx = jax.lax.top_k(logits, TOP_K)
        e_star = jnp.max(topk_idx, axis=-1)
        out = jnp.zeros_like(flat_x)
        for i in range(NUM_EXPERTS):
            h = jax.nn.gelu(flat_x @ w1[i] + b1[i], approximate=False)
            y = h @ w2[i] + b2[i]
            out = jnp.where((e_star == i)[:, None], y, out)
        return (TOP_K * out).reshape(B, N, C)
    x = L0_attn_x
    xn = _layernorm(x, axis=-1)
    s = _L0_attn_ref(xn, L0_attn_wq, L0_attn_w_kv_down, L0_attn_w_k_up, L0_attn_w_v_up, L0_attn_wo)
    g = _silu(_L0_ffn_ref(xn, L0_ffn_gate_w, L0_ffn_gate_b, L0_ffn_w1, L0_ffn_b1, L0_ffn_w2, L0_ffn_b2))
    x = x + s * g
    return x

_drawn_inputs = setup_inputs


def setup_inputs(seed=0):
    import zlib

    import numpy as np

    out = dict(_drawn_inputs(seed))
    spreads = {}
    factors = {'L0_ffn_gate_b': 3.758, 'L0_ffn_b1': 26.195, 'L0_ffn_b2': 8.0}
    for name, (base, spread) in spreads.items():
        noise = np.random.default_rng([zlib.crc32(name.encode()), seed]).standard_normal(out[name].shape)
        drawn = base * np.exp(spread * noise) if base else spread * noise
        out[name] = jnp.asarray(drawn.astype(out[name].dtype))
    for name, factor in factors.items():
        out[name] = (out[name] * factor).astype(out[name].dtype)
    return out
```

```python
from contextlib import ExitStack

import numpy as np

import concourse.bass as bass
from concourse import mybir

F32 = mybir.dt.float32
BF16 = mybir.dt.bfloat16
I32 = mybir.dt.int32
U32 = mybir.dt.uint32
ALU = mybir.AluOpType
ACT = mybir.ActivationFunctionType
X_AXIS = mybir.AxisListType.X

P = 128
B, S, C = 8, 256, 128
NT = B * S // P
TPB = S // P
H, HD = 16, 64
HALF = HD // 2
LAT = 64
NG = 4
HPG = H // NG
NP = H // 2
NI = 2 * NG
E, FF = 8, 512
FB = FF // P
TOP_K = 2
NR = NT + E - 2
B1W = E * FF // P
BW = B1W + E * C // P
LN_EPS = 1e-5
NEG = -1e30
SW = P + S
RG = 4


def host_constants():
    f = np.float32
    inv = (f(1.0) / f(10000.0) ** (np.arange(0, HD, 2, dtype=f) / f(HD))).astype(f)
    ang = np.arange(S, dtype=f)[None, :] * np.tile(inv, HPG)[:, None]
    cos, sin = np.cos(ang).astype(f), np.sin(ang).astype(f)
    k = np.arange(P)
    rot = np.stack([np.concatenate([cos, -sin], 1), np.concatenate([sin, cos], 1)], 1)
    e = np.arange(E, dtype=f)
    return {
        "c_rot_k": rot.astype(f),
        "c_rot_q": (rot * f(HD ** -0.5)).astype(f),
        "c_ident": np.eye(P, dtype=f),
        "c_mask": np.where(k[None, :] > k[:, None], f(NEG), f(0.0)).astype(f),
        "c_before": (k[:, None] < k[None, :]).astype(f),
        "c_expert": np.broadcast_to(e, (P, NT, E)).astype(f),
        "c_excl": np.broadcast_to((e[None, :] < e[:, None]).astype(f), (P, E, E)).copy(),
        "c_incl": np.broadcast_to((e[None, :] <= e[:, None]).astype(f), (P, E, E)).copy(),
        "c_tile": np.broadcast_to(np.arange(NR, dtype=f)[:, None], (P, NR, E)).copy(),
    }


def build(nc, x, wqT, w_down, w_downT, w_kupT, w_vup, woT, gate_w, gate_b, w1, b1, w2, b2,
          c_rot_k, c_rot_q, c_ident, c_mask, c_before, c_expert, c_excl, c_incl, c_tile, out):
    with ExitStack() as ctx:
        def sb(name, shape, dt=F32):
            return ctx.enter_context(nc.sbuf_tensor(name, shape, dt))

        def sem(name):
            return ctx.enter_context(nc.semaphore(name))

        bank = [ctx.enter_context(nc.psum_tensor(f"bank{i}", [P, 512], F32)) for i in range(8)]

        sorted_x = nc.dram_tensor("sorted_x", [NR * P, C], F32).ap()
        sorted_g = nc.dram_tensor("sorted_g", [NR * P, C], F32).ap()

        ident = sb("ident", [P, P])
        mask = sb("mask", [P, SW])
        x_sb = sb("x_sb", [P, NT, C])
        xn = sb("xn", [P, NT, C])
        xnT = sb("xnT", [P, NT * P])
        gate = sb("gate", [P, NT, C])
        rot_q = sb("rot_q", [P, 2, 2 * S])
        rot_k = sb("rot_k", [P, 2, 2 * S])
        wq_sb = sb("wq_sb", [P, H * HD])
        wk_sb = sb("wk_sb", [P, H * HD])
        wdn = sb("wdn", [LAT, C])
        wdnT = sb("wdnT", [C, LAT])
        wkup = sb("wkup", [LAT, H * HD])
        wv_sb = sb("wv_sb", [P, NP, LAT])
        wo_sb = sb("wo_sb", [P, NP, C])
        vo_sb = sb("vo_sb", [P, NP, C])
        lat_all = sb("lat_all", [P, NT, LAT])
        gw = sb("gw", [C, E])
        gb = sb("gb", [P, E])
        cex = sb("cex", [P, NT, E])
        cexcl = sb("cexcl", [P, E, E])
        cincl = sb("cincl", [P, E, E])
        ctile = sb("ctile", [1, NR, E])
        cbef = sb("cbef", [P, P])
        cbef16 = sb("cbef16", [P, P], BF16)
        ones16 = sb("ones16", [P, P], BF16)
        halfneg = sb("halfneg", [P, NT])
        pos = sb("pos", [P, NT], U32)
        tile_e = sb("tile_e", [1, NR], I32)

        w_in = sem("w_in")
        c_in = sem("c_in")
        x_in = sem("x_in")

        with ExitStack() as ph:
            def sbp(name, shape, dt=F32):
                return ph.enter_context(nc.sbuf_tensor(name, shape, dt))

            def semp(name):
                return ph.enter_context(nc.semaphore(name))

            st6 = sbp("st6", [P, NT, 6])
            mv = sbp("mv", [P, NT, 2])
            veps = sbp("veps", [P, NT])
            rstd = sbp("rstd", [P, NT])
            lg = sbp("lg", [P, NT, E])
            top = sbp("top", [P, NT, E])
            topi = sbp("topi", [P, NT, E], U32)
            topf = sbp("topf", [P, NT, 2])
            estar = sbp("estar", [P, NT])
            hot = sbp("hot", [P, NT, E])
            hot16 = sbp("hot16", [P, NT, E], BF16)
            cnt_i = sbp("cnt_i", [P, E], I32)
            tiles_i = sbp("tiles_i", [P, E], I32)
            tiles_f = sbp("tiles_f", [P, E])
            prod = sbp("prod", [P, 2, E, E])
            excl = sbp("excl", [P, E])
            incl = sbp("incl", [P, E])
            base = sbp("base", [P, E])
            rank = sbp("rank", [P, NT, E])
            rank2 = sbp("rank2", [P, NT, E])
            posf = sbp("posf", [P, NT])
            cmp = sbp("cmp", [1, NR, E])
            tef = sbp("tef", [1, NR])
            zeros = sbp("zeros", [P, NR * C])

            dch = semp("dch")
            var_ready = semp("var_ready")
            rstd_ready = semp("rstd_ready")
            xn_ready = semp("xn_ready")
            xT_done = semp("xT_done")
            xT_copied = semp("xT_copied")
            lg_done = semp("lg_done")
            hot_ready = semp("hot_ready")
            cnt_done = semp("cnt_done")
            pos_ready = semp("pos_ready")
            zero_ready = semp("zero_ready")
            zero_out = semp("zero_out")
            scattered = semp("scattered")
            cast_ready = semp("cast_ready")
            wk_done = semp("wk_done")
            vo_done = semp("vo_done")
            lat_done = semp("lat_done")
            evac = semp("evac")

            block = ph.enter_context(nc.Block())

            @block.sync
            def _(sp):
                xv = x.rearrange("b (n p) c -> p (b n) c", p=P)
                for q in range(4):
                    n = slice(q * NT // 4, (q + 1) * NT // 4)
                    sp.dma_start(x_sb[:, n, :], xv[:, n, :]).then_inc(x_in, 16)
                for dst, src in ((ident, c_ident), (gw, gate_w), (cex, c_expert),
                                 (cexcl, c_excl), (cincl, c_incl), (cbef, c_before)):
                    sp.dma_start(dst[:], src).then_inc(c_in, 16)
                sp.dma_start(ctile[:], c_tile[0:1]).then_inc(c_in, 16)
                sp.dma_start(gb[:], gate_b.rearrange("(a e) -> a e", a=1).broadcast_to([P, E])).then_inc(c_in, 16)
                for dst, src in ((wdn, w_down), (wdnT, w_downT), (wkup, w_kupT), (wq_sb, wqT),
                                 (wv_sb, w_vup), (wo_sb, woT), (rot_q, c_rot_q), (rot_k, c_rot_k)):
                    sp.dma_start(dst[:], src).then_inc(w_in, 16)
                sp.dma_start(mask[:, 0:P], c_mask).then_inc(w_in, 16)
                sp.dma_start(mask[:, 2 * P:3 * P], c_mask).then_inc(w_in, 16)
                sp.wait_ge(zero_ready, 1)
                sp.dma_start(sorted_x.rearrange("(j p) c -> p j c", p=P),
                             zeros[:].rearrange("p (j c) -> p j c", c=C)).then_inc(zero_out, 16)

            @block.gpsimd
            def _(pool):
                pool.memset(zeros[:], 0.0).then_inc(zero_ready, 1)
                pool.memset(halfneg[:], -0.5)
                pool.memset(mask[:, P:2 * P], 0.0).then_inc(cast_ready, 1)
                pool.wait_ge(cast_ready, 1)
                pool.wait_ge(var_ready, 1)
                pool.tensor_tensor(rstd[:], veps[:], halfneg[:], op=ALU.pow).then_inc(rstd_ready, 1)
                pool.wait_ge(zero_out, 16)
                pool.wait_ge(pos_ready, 1)
                for n in range(NT):
                    pool.indirect_dma_start(
                        out=sorted_x, out_offset=bass.IndirectOffsetOnAxis(ap=pos[:, n:n + 1], axis=0),
                        in_=xn[:, n, :], in_offset=None).then_inc(scattered, 16)
                pool.wait_ge(scattered, 16 * NT)

            @block.vector
            def _(dve):
                step = [0]

                def then(ins):
                    step[0] += 1
                    ins.then_inc(dch, 1)
                    dve.wait_ge(dch, step[0])

                dve.memset(ones16[:], 1.0)
                dve.wait_ge(x_in, 64)
                for n in range(NT):
                    last = dve.bn_stats(st6[:, n, :], x_sb[:, n, :])
                then(last)
                for n in range(NT):
                    last = dve.bn_aggr(mv[:, n, :], st6[:, n, :])
                then(last)
                dve.tensor_scalar(veps[:], mv[:, :, 1], LN_EPS, None, ALU.add).then_inc(var_ready, 1)
                dve.wait_ge(rstd_ready, 1)
                for n in range(NT):
                    dve.tensor_scalar(xn[:, n, :], x_sb[:, n, :], mv[:, n, 0:1], rstd[:, n:n + 1],
                                      ALU.subtract, ALU.mult).then_inc(xn_ready, 1)
                dve.wait_ge(c_in, 16 * 8)
                dve.tensor_copy(cbef16[:], cbef[:]).then_inc(hot_ready, 1)

                dve.wait_ge(lg_done, 1)
                then(dve.tensor_tensor(lg[:], bank[4][:, 0:NT * E].rearrange("p (n e) -> p n e", e=E),
                                       gb[:].unsqueeze(1).broadcast_to([P, NT, E]), op=ALU.add))
                for n in range(NT):
                    last = dve.max(top[:, n, :], lg[:, n, :])
                then(last)
                for n in range(NT):
                    last = dve.max_index(topi[:, n, :], top[:, n, :], lg[:, n, :])
                then(last)
                then(dve.tensor_copy(topf[:], topi[:, :, 0:2]))
                then(dve.tensor_reduce(estar[:], topf[:], X_AXIS, ALU.max))
                then(dve.tensor_tensor(hot[:], cex[:], estar[:].unsqueeze(2).broadcast_to([P, NT, E]),
                                       op=ALU.is_equal))
                dve.tensor_copy(hot16[:], hot[:]).then_inc(hot_ready, 1)

                dve.wait_ge(cnt_done, 1)
                then(dve.tensor_scalar(cnt_i[:], bank[5][:, 0:E], float(P - 1), None, ALU.add))
                then(dve.tensor_scalar(tiles_i[:], cnt_i[:], 7, None, ALU.arith_shift_right))
                then(dve.tensor_copy(tiles_f[:], tiles_i[:]))
                tb = tiles_f[:].unsqueeze(1).broadcast_to([P, E, E])
                dve.tensor_tensor(prod[:, 0], cexcl[:], tb, op=ALU.mult)
                then(dve.tensor_tensor(prod[:, 1], cincl[:], tb, op=ALU.mult))
                dve.tensor_reduce(excl[:], prod[:, 0], X_AXIS, ALU.add)
                then(dve.tensor_reduce(incl[:], prod[:, 1], X_AXIS, ALU.add))
                then(dve.tensor_scalar(base[:], excl[:], float(P), None, ALU.mult))
                then(dve.tensor_tensor(rank[:], bank[6][:, 0:NT * E].rearrange("p (n e) -> p n e", e=E),
                                       base[:].unsqueeze(1).broadcast_to([P, NT, E]), op=ALU.add))
                then(dve.tensor_tensor(rank2[:], rank[:], hot[:], op=ALU.mult))
                then(dve.tensor_reduce(posf[:], rank2[:], X_AXIS, ALU.add))
                dve.tensor_copy(pos[:], posf[:]).then_inc(pos_ready, 1)
                then(dve.tensor_tensor(cmp[:], incl[0:1, :].unsqueeze(1).broadcast_to([1, NR, E]), ctile[:],
                                       op=ALU.is_le))
                then(dve.tensor_reduce(tef[:], cmp[:], X_AXIS, ALU.add))
                then(dve.tensor_scalar(tile_e[:], tef[:], float(E - 1), None, ALU.min))

                dve.wait_ge(wk_done, 1)
                for q in range(2):
                    dve.tensor_copy(wk_sb[:, q * 512:(q + 1) * 512], bank[2 + q][:])
                dve.wait_ge(vo_done, 1)
                for q in range(2):
                    dve.tensor_copy(vo_sb[:, 4 * q:4 * q + 4, :].rearrange("p n c -> p (n c)"), bank[q][:]).then_inc(evac, 1)
                for q in range(2):
                    dve.wait_ge(lat_done, q + 1)
                    dve.tensor_copy(lat_all[:, 8 * q:8 * q + 8, :].rearrange("p n c -> p (n c)"), bank[4 + q][:])

            @block.scalar
            def _(act):
                for q in range(NT // 4):
                    act.wait_ge(xT_done, q + 1)
                    act.copy(xnT[:, q * 512:(q + 1) * 512], bank[q][:]).then_inc(xT_copied, 1)

            @block.tensor
            def _(pe):
                pe.wait_ge(c_in, 16 * 8)
                for n in range(NT):
                    pe.wait_ge(xn_ready, n + 1)
                    t = pe.transpose(bank[n // 4][:, (n % 4) * P:(n % 4 + 1) * P], xn[:, n, :], ident[:])
                    if n % 4 == 3:
                        t.then_inc(xT_done, 1)
                for n in range(NT):
                    pe.wait_ge(xT_copied, n // 4 + 1)
                    m = pe.matmul(bank[4][:, n * E:(n + 1) * E], xnT[:, n * P:(n + 1) * P], gw[:],
                                  start=True, stop=True)
                m.then_inc(lg_done, 1)
                pe.wait_ge(w_in, 16 * 10)
                for q in range(2):
                    m = pe.matmul(bank[2 + q][:], wdn[:], wkup[:, q * 512:(q + 1) * 512], start=True, stop=True)
                m.then_inc(wk_done, 1)
                for h in range(H):
                    r = slice(HD * (h % 2), HD * (h % 2) + HD)
                    m = pe.matmul(bank[h // 8][r, (h // 2 % 4) * C:(h // 2 % 4 + 1) * C], wv_sb[r, h // 2, :],
                                  wo_sb[r, h // 2, :], start=True, stop=True)
                m.then_inc(vo_done, 1)
                pe.wait_ge(hot_ready, 2)
                pe.matmul(bank[6][:, 0:NT * E], cbef16[:], hot16[:].rearrange("p n e -> p (n e)"),
                          start=True, stop=False, skip_group_check=True)
                for n in range(NT - 1):
                    r = NT - 1 - n
                    pe.matmul(bank[6][:, (n + 1) * E:NT * E].rearrange("p (n e) -> p n e", e=E), ones16[:],
                              hot16[:, n:n + 1, :].broadcast_to([P, r, E]),
                              start=False, stop=(n == NT - 2), skip_group_check=True)
                for n in range(NT):
                    m = pe.matmul(bank[5][:, 0:E], ones16[:], hot16[:, n, :], start=(n == 0), stop=(n == NT - 1))
                m.then_inc(cnt_done, 1)
                pe.wait_ge(pos_ready, 1)
                pe.wait_ge(evac, 2)
                for n in range(NT):
                    m = pe.matmul(bank[4 + n // 8][:, (n % 8) * LAT:(n % 8 + 1) * LAT], xnT[:, n * P:(n + 1) * P],
                                  wdnT[:], start=True, stop=True)
                    if n % 8 == 7:
                        m.then_inc(lat_done, 1)

        with ExitStack() as ph:
            def sbp(name, shape, dt=F32):
                return ph.enter_context(nc.sbuf_tensor(name, shape, dt))

            def semp(name):
                return ph.enter_context(nc.semaphore(name))

            w1_sb = sbp("w1_sb", [C, E * FF])
            w2_sb = sbp("w2_sb", [P, FB, E, C])
            bias_in = sbp("bias_in", [P, BW])
            bias_rest = sbp("bias_rest", [P, 2, BW])
            bias_parts = sbp("bias_parts", [P, 3, BW], BF16)
            b1_sb = sbp("b1_sb", [3, E * FF], BF16)
            b2_sb = sbp("b2_sb", [3, E * C], BF16)
            xs = sbp("xs", [P, 2, C])
            xsT = sbp("xsT", [P, 2, P])
            hid = sbp("hid", [P, 2, FF])
            hidT = sbp("hidT", [P, 2, FB, P])
            z = sbp("z", [P, NR, C])

            f_in = semp("f_in")
            fb_in = semp("fb_in")
            b_split = semp("b_split")
            fb_spread = semp("fb_spread")
            xs_in = [semp(f"xs_in{i}") for i in range(2)]
            xsT_done = semp("xsT_done")
            xsT_ready = semp("xsT_ready")
            h_done = semp("h_done")
            hid_ready = semp("hid_ready")
            hidT_done = semp("hidT_done")
            hidT_ready = semp("hidT_ready")
            y_done = semp("y_done")
            z_ready = semp("z_ready")
            g_ready = semp("g_ready")
            g_out = semp("g_out")
            g_in = semp("g_in")
            b_link = semp("b_link")

            def wait(eng, s, v):
                if not isinstance(v, int) or v > 0:
                    eng.wait_ge(s, v)

            def over_pairs(eng, body):
                body(0)
                with eng.Fori(1, NR // 2) as m:
                    body(2 * m)

            block = ph.enter_context(nc.Block())

            @block.sync
            def _(sp):
                sp.dma_start(bias_in[:, 0:B1W], b1.rearrange("e (q f) -> (e q) f", f=B1W)).then_inc(fb_in, 16)
                sp.dma_start(bias_in[:, B1W:BW], b2.rearrange("e (q f) -> (e q) f", f=BW - B1W)).then_inc(fb_in, 16)
                sp.dma_start(w1_sb[:].rearrange("p (e f) -> p e f", e=E), w1.rearrange("e c f -> c e f")).then_inc(f_in, 16)
                for k in range(FB):
                    sp.dma_start(w2_sb[:, k], w2.rearrange("e (k p) c -> k p e c", p=P)[k]).then_inc(f_in, 16)
                sp.wait_ge(b_split, 1)
                for i in range(3):
                    sp.dma_start(b1_sb[i:i + 1, :].rearrange("a (p f) -> a p f", f=B1W), bias_parts[:, i, 0:B1W]).then_inc(fb_spread, 16)
                    sp.dma_start(b2_sb[i:i + 1, :].rearrange("a (p f) -> a p f", p=P), bias_parts[:, i, B1W:BW]).then_inc(fb_spread, 16)

                def pair(j):
                    for i in range(2):
                        wait(sp, xsT_done, j + i - 1)
                        sp.dma_start(xs[:, i, :], sorted_x[bass.ds((j + i) * P, P), :]).then_inc(xs_in[i], 16)
                over_pairs(sp, pair)

                for q in range(2):
                    n = slice(q * NR // 2, (q + 1) * NR // 2)
                    sp.wait_ge(g_ready, q + 1)
                    sp.dma_start(sorted_g.rearrange("(j p) c -> p j c", p=P)[:, n, :], z[:, n, :]).then_inc(g_out, 16)

            @block.gpsimd
            def _(pool):
                pool.wait_ge(g_out, 32)
                for n in range(NT):
                    pool.indirect_dma_start(
                        out=gate[:, n, :], out_offset=None, in_=sorted_g,
                        in_offset=bass.IndirectOffsetOnAxis(ap=pos[:, n:n + 1], axis=0)).then_inc(g_in, 16)
                pool.wait_ge(g_in, 16 * NT)

            @block.tensor
            def _(pe):
                pe.wait_ge(fb_spread, 96)
                pe.wait_ge(f_in, 16 * (1 + FB))

                def pair(j):
                    e = [pe.value_load(tile_e[0:1, bass.ds(j + i, 1)], min_val=0, max_val=E - 1) for i in range(2)]
                    for i in range(2):
                        wait(pe, xs_in[i], j * 8 + 16)
                        wait(pe, xsT_ready, j)
                        pe.transpose(bank[0][:, i * P:(i + 1) * P], xs[:, i, :], ident[:]).then_inc(xsT_done, 1)
                    for i in range(2):
                        pe.wait_ge(xsT_ready, j + 2)
                        wait(pe, hid_ready, j + i - 1)
                        pe.matmul(bank[1 + i][:], ones16[0:3, :], b1_sb[:, bass.ds(e[i] * FF, FF)], start=True, stop=False)
                        pe.matmul(bank[1 + i][:], xsT[:, i, :], w1_sb[:, bass.ds(e[i] * FF, FF)],
                                  start=False, stop=True).then_inc(h_done, 1)
                    for i in range(2):
                        pe.wait_ge(hid_ready, j + i + 1)
                        wait(pe, hidT_ready, j + i - 1)
                        for k in range(FB):
                            t = pe.transpose(bank[3 + i][:, k * P:(k + 1) * P], hid[:, i, k * P:(k + 1) * P], ident[:])
                        t.then_inc(hidT_done, 1)
                    for i in range(2):
                        pe.wait_ge(hidT_ready, j + i + 1)
                        wait(pe, z_ready, j + i - 1)
                        pe.matmul(bank[5 + i][:, 0:C], ones16[0:3, :], b2_sb[:, bass.ds(e[i] * C, C)], start=True, stop=False)
                        for k in range(FB):
                            m = pe.matmul(bank[5 + i][:, 0:C], hidT[:, i, k, :],
                                          w2_sb[:, k, :, :].rearrange("p e c -> p (e c)")[:, bass.ds(e[i] * C, C)],
                                          start=False, stop=(k == FB - 1))
                        m.then_inc(y_done, 1)
                over_pairs(pe, pair)

            @block.scalar
            def _(act):
                def pair(j):
                    for i in range(2):
                        act.wait_ge(h_done, j + i + 1)
                        wait(act, hidT_done, j + i - 1)
                        act.activation(hid[:, i, :], bank[1 + i][:], ACT.Gelu).then_inc(hid_ready, 1)
                over_pairs(act, pair)
                for q in range(2):
                    n = slice(q * NR // 2, (q + 1) * NR // 2)
                    act.wait_ge(z_ready, (q + 1) * NR // 2)
                    act.activation(z[:, n, :], z[:, n, :], ACT.Silu).then_inc(g_ready, 1)

            @block.vector
            def _(dve):
                step = [0]

                def then(ins):
                    step[0] += 1
                    ins.then_inc(b_link, 1)
                    dve.wait_ge(b_link, step[0])

                dve.wait_ge(fb_in, 32)
                then(dve.tensor_copy(bias_parts[:, 0, :], bias_in[:]))
                then(dve.tensor_tensor(bias_rest[:, 0, :], bias_in[:], bias_parts[:, 0, :], op=ALU.subtract))
                then(dve.tensor_copy(bias_parts[:, 1, :], bias_rest[:, 0, :]))
                then(dve.tensor_tensor(bias_rest[:, 1, :], bias_rest[:, 0, :], bias_parts[:, 1, :], op=ALU.subtract))
                last = dve.tensor_copy(bias_parts[:, 2, :], bias_rest[:, 1, :])
                last.then_inc(b_split, 1)

                def pair(j):
                    dve.wait_ge(xsT_done, j + 2)
                    wait(dve, h_done, j)
                    dve.tensor_copy(xsT[:].rearrange("p i n -> p (i n)"), bank[0][:, 0:2 * P]).then_inc(xsT_ready, 2)
                    for i in range(2):
                        dve.wait_ge(hidT_done, j + i + 1)
                        wait(dve, y_done, j + i - 1)
                        dve.tensor_copy(hidT[:, i].rearrange("p k n -> p (k n)"), bank[3 + i][:]).then_inc(hidT_ready, 1)
                    for i in range(2):
                        dve.wait_ge(y_done, j + i + 1)
                        dve.tensor_scalar(z[:, bass.ds(j + i, 1), :].rearrange("p a c -> p (a c)"), bank[5 + i][:, 0:C],
                                          float(TOP_K), None, ALU.mult).then_inc(z_ready, 1)
                over_pairs(dve, pair)

        with ExitStack() as ph:
            def sbp(name, shape, dt=F32):
                return ph.enter_context(nc.sbuf_tensor(name, shape, dt))

            def semp(name):
                return ph.enter_context(nc.semaphore(name))

            sb_rot = sbp("sb_rot", [P, 2, 2, 2 * S])
            staged = sbp("staged", [P, 2, 2, 2, S])
            qk_sb = sbp("qk_sb", [P, 2, NP, S])
            q_sb, k_sb = qk_sb[:, 0], qk_sb[:, 1]
            masked = sbp("masked", [P, RG, SW])
            negmax = sbp("negmax", [P, RG, 2])
            rowsum = sbp("rowsum", [P, RG, 2])
            rden = sbp("rden", [P, RG, 2])
            pexp = sbp("pexp", [P, 2, SW])
            probs = sbp("probs", [P, 2, SW])
            probsT = sbp("probsT", [P, 2, SW])
            lat = sbp("lat", [P, 2, LAT])
            ctxT = sbp("ctxT", [P, NP, S])
            gated = sbp("gated", [P, 2, C])
            res = sbp("res", [P, 2, C])

            proj_done = semp("proj_done")
            rope_done = semp("rope_done")
            staged_ready = semp("staged_ready")
            qk_in = [semp(f"qk_in{i}") for i in range(NG)]
            scores_done = semp("scores_done")
            masked_ready = semp("masked_ready")
            exp_done = semp("exp_done")
            rden_ready = semp("rden_ready")
            probs_ready = semp("probs_ready")
            probsT_done = semp("probsT_done")
            probsT_ready = semp("probsT_ready")
            pv_done = semp("pv_done")
            ctx_ready = semp("ctx_ready")
            lat_ready = semp("lat_ready")
            y_done = semp("att_y_done")
            gated_ready = semp("gated_ready")
            res_ready = semp("res_ready")
            out_done = semp("out_done")
            scale_turn = semp("scale_turn")
            store_turn = semp("store_turn")

            s_bank, t_bank, j_bank, o_bank, y_bank = bank[0:2], bank[2:4], bank[4:6], bank[6], bank[7]

            def wait(eng, s, v):
                if not isinstance(v, int) or v > 0:
                    eng.wait_ge(s, v)

            def over_batches(eng, prologue, body):
                prologue()
                body(0, False)
                with eng.Fori(1, B - 1) as b:
                    body(b, False)
                body(B - 1, True)

            block = ph.enter_context(nc.Block())

            @block.tensor
            def _(pe):
                def project(b, n):
                    g, w = n // 2, (wq_sb, wk_sb)[n % 2]
                    wait(pe, rope_done, NI * b + n - 1)
                    for half in range(2):
                        m = pe.matmul(j_bank[n % 2][:, half * S:(half + 1) * S],
                                      w[:, (2 * g + half) * P:(2 * g + half + 1) * P], xnT[:, bass.ds(b * S, S)],
                                      start=True, stop=True)
                    m.then_inc(proj_done, 1)

                def scores(b, h):
                    r, p = slice(HD * (h % 2), HD * (h % 2) + HD), h // 2
                    if h % HPG == 0:
                        pe.wait_ge(qk_in[h // HPG], 128 * b + 128)
                    wait(pe, masked_ready, H * b + h - 1)
                    pe.matmul(s_bank[h % 2][:, 0:P], q_sb[r, p, 0:P], k_sb[r, p, 0:P], start=True, stop=True)
                    pe.matmul(s_bank[h % 2][:, P:SW], q_sb[r, p, P:S], k_sb[r, p, :],
                              start=True, stop=True).then_inc(scores_done, 1)

                def turn(b, h):
                    pe.wait_ge(probs_ready, H * b + h + 1)
                    wait(pe, probsT_ready, H * b + h - 1)
                    for k in range(3):
                        t = pe.transpose(t_bank[h % 2][:, k * P:(k + 1) * P], probs[:, h % 2, k * P:(k + 1) * P], ident[:])
                    t.then_inc(probsT_done, 1)

                def values(b, h):
                    o = o_bank[HD * (h % 2):HD * (h % 2) + HD, 0:S]
                    if h == 0:
                        pe.wait_ge(lat_ready, b + 1)
                    if h % 2 == 0:
                        wait(pe, ctx_ready, NP * b + h // 2)
                    pe.wait_ge(probsT_ready, H * b + h + 1)
                    pe.matmul(o, lat[:, 0, :], probsT[:, h % 2, 0:S], start=True, stop=False)
                    pe.matmul(o[:, P:S], lat[:, 1, :], probsT[:, h % 2, S:SW], start=False,
                              stop=True).then_inc(pv_done, 1)

                def output(b, p):
                    if p == 0:
                        wait(pe, gated_ready, b)
                    pe.wait_ge(ctx_ready, NP * b + p + 1)
                    for i in range(2):
                        m = pe.matmul(y_bank[:, i * C:(i + 1) * C], ctxT[:, p, i * P:(i + 1) * P], vo_sb[:, p, :],
                                      start=(p == 0 and i == 0), stop=(p == NP - 1), skip_group_check=True)
                    if p == NP - 1:
                        m.then_inc(y_done, 1)

                def prologue():
                    for n in range(NI):
                        project(0, n)
                    for h in range(3):
                        scores(0, h)

                def body(b, last):
                    for h in range(H):
                        if h + 3 < H:
                            scores(b, h + 3)
                        elif not last:
                            scores(b + 1, h + 3 - H)
                        turn(b, h)
                        if h > 0:
                            values(b, h - 1)
                        if h % 2 and h >= 3:
                            output(b, h // 2 - 1)
                        if h % 2 and not last and h < H - 1:
                            project(b + 1, h // 2)
                    values(b, H - 1)
                    if not last:
                        project(b + 1, NI - 1)
                    output(b, NP - 1)
                over_batches(pe, prologue, body)

            @block.vector
            def _(dve):
                def rotate(b, n):
                    dve.wait_ge(proj_done, NI * b + n + 1)
                    wait(dve, staged_ready, NI * b + n - 1)
                    for r in range(2):
                        m = dve.tensor_tensor(sb_rot[:, n % 2, r, :], j_bank[n % 2][:], (rot_q, rot_k)[n % 2][:, r, :],
                                              op=ALU.mult)
                    m.then_inc(rope_done, 1)

                def row_max(b, h):
                    s, m = s_bank[h % 2], masked[:, h % RG]
                    for i, c in enumerate((slice(0, P), slice(P, SW))):
                        t = dve.tensor_tensor_reduce(m[:, c], s[:, c], mask[:, c], -1.0, -NEG * 1e8, ALU.add, ALU.min,
                                                     negmax[:, h % RG, i:i + 1])
                    t.then_inc(masked_ready, 1)

                def denominators(b, h, ahead=True):
                    dve.wait_ge(exp_done, H * b + h + 1)
                    if ahead:
                        dve.wait_ge(scores_done, H * b + h + 3)
                    dve.reciprocal(rden[:, h % RG, :], rowsum[:, h % RG, :]).then_inc(rden_ready, 1)

                def prologue():
                    for n in range(NI):
                        rotate(0, n)
                    for h in range(3):
                        dve.wait_ge(scores_done, h + 1)
                        row_max(0, h)
                    denominators(0, 0)

                def body(b, last):
                    for h in range(H):
                        if h + 1 < H:
                            denominators(b, h + 1, ahead=(h + 3 < H or not last))
                        elif not last:
                            denominators(b + 1, 0)
                        if h + 3 < H:
                            row_max(b, h + 3)
                        elif not last:
                            row_max(b + 1, h + 3 - H)
                        if h == 0:
                            wait(dve, pv_done, H * b)
                            dve.tensor_copy(lat[:], lat_all[:, bass.ds(2 * b, 2), :]).then_inc(lat_ready, 1)
                        if h % 2 == 0 and h > 0 and not last:
                            rotate(b + 1, h // 2 - 1)
                    if not last:
                        rotate(b + 1, NI - 1)
                    dve.wait_ge(y_done, b + 1)
                    wait(dve, res_ready, b)
                    dve.tensor_tensor(gated[:].rearrange("p n c -> p (n c)"), y_bank[:, 0:2 * C],
                                      gate[:, bass.ds(2 * b, 2), :].rearrange("p n c -> p (n c)"),
                                      op=ALU.mult).then_inc(gated_ready, 1)
                    dve.wait_ge(gated_ready, b + 1)
                    wait(dve, out_done, 16 * b)
                    dve.tensor_tensor(res[:], gated[:], x_sb[:, bass.ds(2 * b, 2), :], op=ALU.add).then_inc(res_ready, 1)
                over_batches(dve, prologue, body)

            @block.scalar
            def _(act):
                def exponentials(b, h):
                    act.wait_ge(masked_ready, H * b + h + 1)
                    wait(act, probs_ready, H * b + h - 1)
                    for i, c in enumerate((slice(0, P), slice(P, SW))):
                        e = act.activation(pexp[:, h % 2, c], masked[:, h % RG, c], ACT.Exp, bias=negmax[:, h % RG, i:i + 1],
                                           scale=-1.0, accum_out=rowsum[:, h % RG, i:i + 1])
                    e.then_inc(exp_done, 1)

                def probs_out(b, h):
                    act.wait_ge(probsT_done, H * b + h + 1)
                    wait(act, pv_done, H * b + h - 1)
                    act.copy(probsT[:, h % 2, :], t_bank[h % 2][:, 0:SW]).then_inc(probsT_ready, 1)

                def ctx_out(b, p):
                    act.wait_ge(pv_done, H * b + 2 * p + 2)
                    if p == 0:
                        wait(act, y_done, b)
                    act.copy(ctxT[:, p, :], o_bank[:, 0:S]).then_inc(ctx_ready, 1)

                def prologue():
                    for h in range(2):
                        exponentials(0, h)

                def body(b, last):
                    for h in range(H):
                        if h + 2 < H:
                            exponentials(b, h + 2)
                        elif not last:
                            exponentials(b + 1, h + 2 - H)
                        probs_out(b, h)
                        if h % 2 == 0 and h > 0:
                            ctx_out(b, h // 2 - 1)
                    ctx_out(b, NP - 1)
                over_batches(act, prologue, body)

            @block.gpsimd
            def _(pool):
                def rotated(b, n):
                    pool.wait_ge(rope_done, NI * b + n + 1)
                    g = n // 2
                    if g >= 2:
                        pool.wait_ge(qk_in[g - 2], 128 * b + 128)
                    else:
                        wait(pool, qk_in[g + 2], 128 * b)
                    pool.tensor_tensor(staged[:, g % 2, :, n % 2, :], sb_rot[:, n % 2, :, 0:S], sb_rot[:, n % 2, :, S:2 * S],
                                       op=ALU.add).then_inc(staged_ready, 1)

                def scale(b, h):
                    pool.wait_ge(rden_ready, H * b + h + 1)
                    wait(pool, probsT_done, H * b + h - 1)
                    pool.sem_inc(scale_turn, 1)
                    for i, c in enumerate((slice(0, P), slice(P, SW))):
                        m = pool.tensor_scalar(probs[:, h % 2, c], pexp[:, h % 2, c], rden[:, h % RG, i:i + 1], 1.0,
                                               ALU.mult, ALU.mult)
                    m.then_inc(probs_ready, 1)

                def prologue():
                    for n in range(NI):
                        rotated(0, n)
                    scale(0, 0)

                def body(b, last):
                    for h in range(H):
                        if h + 1 < H:
                            scale(b, h + 1)
                        elif not last:
                            scale(b + 1, 0)
                        if h % 2 == 0 and h > 0 and not last:
                            rotated(b + 1, h // 2 - 1)
                    if not last:
                        rotated(b + 1, NI - 1)
                over_batches(pool, prologue, body)

            @block.sync
            def _(sp):
                def place(b, g):
                    sp.wait_ge(staged_ready, NI * b + 2 * g + 2)
                    sp.sem_inc(store_turn, 1)
                    wait(sp, scores_done, H * b + HPG * (g + 1) - H)
                    for hh in range(HPG):
                        for half in range(2):
                            to = HD * (hh % 2) + HALF * half
                            sp.dma_start(qk_sb[to:to + HALF, :, 2 * g + hh // 2, :],
                                         staged[HALF * hh:HALF * (hh + 1), g % 2, half]).then_inc(qk_in[g], 16)

                def prologue():
                    for g in range(NG):
                        place(0, g)

                def body(b, last):
                    if not last:
                        for g in range(NG):
                            place(b + 1, g)
                    sp.wait_ge(res_ready, b + 1)
                    sp.sem_inc(store_turn, 1)
                    ov = out.rearrange("b (n p) c -> b p n c", p=P)[bass.ds(b, 1)].rearrange("a p n c -> (a p) n c")
                    sp.dma_start(ov, res[:]).then_inc(out_done, 16)
                over_batches(sp, prologue, body)
                sp.wait_ge(out_done, 16 * B)


def kernel(**inputs):
    import concourse.bacc as bacc
    from concourse.bass_utils import run_bass_kernel_spmd

    g = {k: np.asarray(v) for k, v in inputs.items()}
    by_half = lambda w: w.reshape(NG, HPG, 2, HALF, -1).transpose(4, 0, 2, 1, 3).reshape(w.shape[1], H * HD)
    arrays = {
        "x": g["L0_attn_x"],
        "wqT": by_half(g["L0_attn_wq"]),
        "w_down": g["L0_attn_w_kv_down"],
        "w_downT": g["L0_attn_w_kv_down"].T,
        "w_kupT": by_half(g["L0_attn_w_k_up"]),
        "w_vup": g["L0_attn_w_v_up"].reshape(NP, 2 * HD, LAT).transpose(1, 0, 2),
        "woT": g["L0_attn_wo"].reshape(C, NP, 2 * HD).transpose(2, 1, 0),
        "gate_w": g["L0_ffn_gate_w"],
        "gate_b": g["L0_ffn_gate_b"],
        "w1": g["L0_ffn_w1"],
        "b1": g["L0_ffn_b1"],
        "w2": g["L0_ffn_w2"],
        "b2": g["L0_ffn_b2"],
        **host_constants(),
    }
    arrays = {k: np.ascontiguousarray(v) for k, v in arrays.items()}
    nc = bacc.Bacc("TRN2", target_bir_lowering=False, num_devices=1)
    aps = {k: nc.dram_tensor(f"in_{k}", v.shape, mybir.dt.from_np(v.dtype), kind="ExternalInput").ap()
           for k, v in arrays.items()}
    out = nc.dram_tensor("out", (B, S, C), F32, kind="ExternalOutput").ap()
    build(nc, **aps, out=out)
    r = run_bass_kernel_spmd(nc, [{f"in_{k}": v for k, v in arrays.items()}], core_ids=[0])
    return r.results[0]["out"]
```

```python
from contextlib import ExitStack

import numpy as np

import concourse.bass as bass
from concourse import mybir

F32 = mybir.dt.float32
F32R = mybir.dt.float32r
BF16 = mybir.dt.bfloat16
I32 = mybir.dt.int32
U32 = mybir.dt.uint32
ALU = mybir.AluOpType
ACT = mybir.ActivationFunctionType
X_AXIS = mybir.AxisListType.X

P = 128
B, S, C = 8, 256, 128
NT = B * S // P
TPB = S // P
H, HD = 16, 64
HALF = HD // 2
LAT = 64
NG = 4
HPG = H // NG
NP = H // 2
NI = 2 * NG
E, FF = 8, 512
FB = FF // P
TOP_K = 2
NR = NT + E - 2
B1W = E * FF // P
BW = B1W + E * C // P
LN_EPS = 1e-5
NEG = -1e30
SW = P + S


def host_constants():
    f = np.float32
    inv = (f(1.0) / f(10000.0) ** (np.arange(0, HD, 2, dtype=f) / f(HD))).astype(f)
    ang = np.arange(S, dtype=f)[None, :] * np.tile(inv, HPG)[:, None]
    cos, sin = np.cos(ang).astype(f), np.sin(ang).astype(f)
    k = np.arange(P)
    e = np.arange(E, dtype=f)
    return {
        "c_rot": np.stack([np.concatenate([cos, -sin], 1), np.concatenate([sin, cos], 1)], 1).astype(f),
        "c_ident": np.eye(P, dtype=f),
        "c_mask": np.where(k[None, :] > k[:, None], f(NEG), f(0.0)).astype(f),
        "c_before": (k[:, None] < k[None, :]).astype(f),
        "c_expert": np.broadcast_to(e, (P, NT, E)).astype(f),
        "c_excl": np.broadcast_to((e[None, :] < e[:, None]).astype(f), (P, E, E)).copy(),
        "c_incl": np.broadcast_to((e[None, :] <= e[:, None]).astype(f), (P, E, E)).copy(),
        "c_tile": np.broadcast_to(np.arange(NR, dtype=f)[:, None], (P, NR, E)).copy(),
    }


def wait(eng, s, v):
    if not isinstance(v, int) or v > 0:
        eng.wait_ge(s, v)


def build(nc, x, wqT, w_downT, w_kupT, w_vup, woT, gate_w, gate_b, w1, b1, w2, b2,
          c_rot, c_ident, c_mask, c_before, c_expert, c_excl, c_incl, c_tile, out):
    with ExitStack() as ctx:
        def sb(name, shape, dt=F32):
            return ctx.enter_context(nc.sbuf_tensor(name, shape, dt))

        def sem(name):
            return ctx.enter_context(nc.semaphore(name))

        bank = [ctx.enter_context(nc.psum_tensor(f"bank{i}", [P, 512], F32)) for i in range(8)]
        s_bank, t_bank, j_bank, o_bank, y_bank = bank[0:2], bank[2:4], bank[4:6], bank[6], bank[7]

        sorted_x = nc.dram_tensor("sorted_x", [NR * P, C], F32).ap()
        sorted_g = nc.dram_tensor("sorted_g", [NR * P, C], F32).ap()

        ident = sb("ident", [P, P])
        mask = sb("mask", [P, SW])
        x_sb = sb("x_sb", [P, NT, C])
        xn = sb("xn", [P, NT, C])
        gate = xn
        xnT_h = sb("xnT_h", [P, NT * P], F32R)
        xnT_l = sb("xnT_l", [P, NT * P], F32R)
        rot = sb("rot", [P, 2, 2 * S])
        wq_h = sb("wq_h", [P, H * HD], F32R)
        wq_l = sb("wq_l", [P, H * HD], F32R)
        wk_h = sb("wk_h", [P, H * HD], F32R)
        wk_l = sb("wk_l", [P, H * HD], F32R)
        vo_sb = sb("vo_sb", [P, NP, C])
        latT = sb("latT", [P, NT * P], F32R)
        lat_all = sb("lat_all", [P, NT, 2, LAT], F32R)
        ones16 = sb("ones16", [P, P], BF16)
        pos = sb("pos", [P, NT], U32)
        tile_e = sb("tile_e", [1, NR], I32)

        w1_sb = sb("w1_sb", [C, E * FF])
        w2_sb = sb("w2_sb", [P, FB, E, C])
        b1_sb = sb("b1_sb", [3, E * FF], BF16)
        b2_sb = sb("b2_sb", [3, E * C], BF16)

        rot_out = sb("rot_out", [P, 2, 2, 2 * S])
        staged = sb("staged", [P, 2, 2, 2, S])
        qk_sb = sb("qk_sb", [P, 2, NP, S])
        masked = sb("masked", [P, 2, SW])
        negmax = sb("negmax", [P, 2, 2])
        rowsum = sb("rowsum", [P, 4, 2])
        rden = sb("rden", [P, 4, 2])
        pexp = sb("pexp", [P, 4, SW])
        probs = sb("probs", [P, 2, SW])
        probsT = sb("probsT", [P, 2, 2, SW], F32R)
        lat = sb("lat", [P, 2, 2, 3 * LAT], F32R)
        ctxT = sb("ctxT", [P, NP, S])
        y_keep = sb("y_keep", [P, 2, C])
        gated = sb("gated", [P, 2, C])
        res = sb("res", [P, 2, C])

        def start_tensors():
            with ExitStack() as ph:
                t = {}
                for name, shape, dt in (
                        ("wdnT", [C, 2 * LAT], F32),
                        ("wdnT_h", [C, 2 * LAT], F32R), ("wdnT_l", [C, 2 * LAT], F32R),
                        ("wv_sb", [P, NP, LAT], F32), ("wo_sb", [P, NP, C], F32),
                        ("gw", [C, E], F32), ("gw_h", [C, E], F32R), ("gw_l", [C, E], F32R), ("gb", [P, E], F32),
                        ("cex", [P, NT, E], F32), ("cexcl", [P, E, E], F32), ("cincl", [P, E, E], F32),
                        ("ctile", [1, NR, E], F32), ("cbef", [P, P], F32), ("cbef16", [P, P], BF16),
                        ("halfneg", [P, NT], F32), ("zeros", [P, C], F32),
                        ("st6", [P, NT, 6], F32), ("mv", [P, NT, 2], F32), ("veps", [P, NT], F32),
                        ("rstd", [P, NT], F32), ("lg", [P, NT, E], F32), ("top", [P, NT, E], F32),
                        ("topi", [P, NT, E], U32), ("topf", [P, NT, 2], F32), ("estar", [P, NT], F32),
                        ("hot", [P, NT, E], F32), ("hot16", [P, NT, E], BF16), ("cnt_i", [P, E], I32),
                        ("tiles_i", [P, E], I32), ("tiles_f", [P, E], F32), ("prod", [P, 2, E, E], F32),
                        ("excl", [P, E], F32), ("incl", [P, E], F32), ("base", [P, E], F32),
                        ("rank", [P, NT, E], F32), ("rank2", [P, NT, E], F32), ("posf", [P, NT], F32),
                        ("cmp", [1, NR, E], F32), ("tef", [1, NR], F32),
                        ("bias_in", [P, BW], F32), ("bias_rest", [P, 2, BW], F32), ("bias_parts", [P, 3, BW], BF16)):
                    t[name] = ph.enter_context(nc.sbuf_tensor(name, shape, dt))
                return t

        T = start_tensors()
        T["wq_in"] = w1_sb[:, 0:H * HD]
        T["wkup"] = w1_sb[:, H * HD:2 * H * HD]
        T["lgT"] = w1_sb[0:E, 2 * H * HD:2 * H * HD + NT * P]
        xsT = sb("xsT", [P, 2, P])
        hid = sb("hid", [P, 2, FF])
        hidT = sb("hidT", [P, 2, FB, P])
        xs = sb("xs", [P, 2, C])
        z = sb("z", [P, NR, C])

        NC_IN = 6

        x_in = [sem(f"x_in{q}") for q in range(4)]
        id_in = sem("id_in")
        c_in = sem("c_in")
        wk_in = sem("wk_in")
        wq_in = sem("wq_in")
        wd_in = sem("wd_in")
        w_in = sem("w_in")
        m_in = sem("m_in")
        f_in = sem("f_in")
        fb_in = sem("fb_in")
        fb_spread = sem("fb_spread")
        zero_ready = sem("zero_ready")
        zero_out = sem("zero_out")
        dve_step = sem("dve_step")
        var_ready = sem("var_ready")
        rstd_ready = sem("rstd_ready")
        xn_ready = sem("xn_ready")
        xT_done = sem("xT_done")
        xT_high = sem("xT_high")
        xT_low = sem("xT_low")
        wsplit_high = sem("wsplit_high")
        wsplit_low = sem("wsplit_low")
        vo_done = sem("vo_done")
        vo_ready = sem("vo_ready")
        lg_done = sem("lg_done")
        lgT_done = sem("lgT_done")
        lgT_ready = sem("lgT_ready")
        latT_done = sem("latT_done")
        latT_high = sem("latT_high")
        latT_low = sem("latT_low")
        lat_turned = sem("lat_turned")
        lat_copied = sem("lat_copied")
        hot_ready = sem("hot_ready")
        cnt_done = sem("cnt_done")
        pos_ready = sem("pos_ready")
        tile_ready = sem("tile_ready")
        bias_split = sem("bias_split")
        scattered = sem("scattered")

        proj_done = sem("proj_done")
        rope_done = sem("rope_done")
        staged_ready = sem("staged_ready")
        qk_in = [sem(f"qk_in{i}") for i in range(NG)]
        scores_done = sem("scores_done")
        masked_ready = sem("masked_ready")
        exp_done = sem("exp_done")
        rden_ready = sem("rden_ready")
        probs_ready = sem("probs_ready")
        probsT_done = sem("probsT_done")
        probsT_high = sem("probsT_high")
        probsT_ready = sem("probsT_ready")
        pv_done = sem("pv_done")
        ctx_ready = sem("ctx_ready")
        lat_ready = sem("lat_ready")
        y_done = sem("y_done")
        y_read = sem("y_read")
        res_ready = sem("res_ready")
        out_done = sem("out_done")
        scale_turn = sem("scale_turn")
        store_turn = sem("store_turn")

        xs_in = [sem(f"xs_in{i}") for i in range(2)]
        xsT_done = sem("xsT_done")
        xsT_ready = sem("xsT_ready")
        h_done = sem("h_done")
        hid_ready = sem("hid_ready")
        hidT_done = sem("hidT_done")
        hidT_ready = sem("hidT_ready")
        e_done = sem("e_done")
        z_ready = sem("z_ready")
        g_ready = sem("g_ready")
        g_out = sem("g_out")
        g_in = sem("g_in")

        POOL_HEADS = 5
        rows = (slice(0, P), slice(P, SW))

        def program(eng, start, body, finish, experts):
            start()
            body(0, False)
            finish(0)
            experts()
            body(1, False)
            with eng.Fori(2, B - 1) as b:
                body(b, False)
            body(B - 1, True)
            finish(B - 1)

        def over_tiles(eng, step):
            step(-1, 1)
            step(0, 0)
            step(1, 1)
            with eng.Fori(1, NR // 2 - 1) as m:
                step(2 * m, 0)
                step(2 * m + 1, 1)
            for t in range(NR - 2, NR + 1):
                step(t, t % 2)

        def has(t, lead):
            return not isinstance(t, int) or 0 <= t + lead < NR

        def at(b, *which):
            return isinstance(b, int) and b in which

        def after(b, h):
            return (b, h + 1) if h + 1 < H else (b + 1, 0)

        def by_pool(b, h):
            return not at(b, 0, 1) or (b == 0 and h < POOL_HEADS)

        block = ctx.enter_context(nc.Block())

        @block.sync
        def _(sp):
            def place(b, g):
                sp.wait_ge(staged_ready, NI * b + 2 * g + 2)
                sp.sem_inc(store_turn, 1)
                wait(sp, scores_done, H * b + HPG * (g + 1) - H)
                for hh in range(HPG):
                    for half in range(2):
                        to = HD * (hh % 2) + HALF * half
                        sp.dma_start(qk_sb[to:to + HALF, :, 2 * g + hh // 2, :],
                                     staged[HALF * hh:HALF * (hh + 1), g % 2, half]).then_inc(qk_in[g], 16)

            def start():
                sp.sem_inc(out_done, 16)
                xv = x.rearrange("b (n p) c -> p (b n) c", p=P)

                def rows_in(q):
                    n = slice(q * NT // 4, (q + 1) * NT // 4)
                    sp.dma_start(x_sb[:, n, :], xv[:, n, :]).then_inc(x_in[q], 16)
                rows_in(0)
                sp.dma_start(T["wdnT"][:], w_downT).then_inc(wd_in, 16)
                sp.dma_start(T["gw"][:], gate_w).then_inc(wd_in, 16)
                sp.dma_start(ident[:], c_ident).then_inc(id_in, 16)
                sp.dma_start(T["wq_in"][:], wqT).then_inc(wq_in, 16)
                sp.dma_start(T["wkup"][:], w_kupT).then_inc(wk_in, 16)
                rows_in(1)
                sp.dma_start(rot[:], c_rot).then_inc(m_in, 16)
                sp.dma_start(T["wv_sb"][:], w_vup).then_inc(w_in, 16)
                sp.dma_start(T["wo_sb"][:], woT).then_inc(w_in, 16)
                for q in range(2, 4):
                    rows_in(q)
                for dst, src in (("cex", c_expert), ("cexcl", c_excl), ("cincl", c_incl),
                                 ("cbef", c_before), ("ctile", c_tile[0:1]),
                                 ("gb", gate_b.rearrange("(a e) -> a e", a=1).broadcast_to([P, E]))):
                    sp.dma_start(T[dst][:], src).then_inc(c_in, 16)
                sp.dma_start(mask[:, 0:P], c_mask).then_inc(m_in, 16)
                sp.dma_start(mask[:, 2 * P:3 * P], c_mask).then_inc(m_in, 16)
                sp.dma_start(T["bias_in"][:, 0:B1W], b1.rearrange("e (q f) -> (e q) f", f=B1W)).then_inc(fb_in, 16)
                sp.dma_start(T["bias_in"][:, B1W:BW], b2.rearrange("e (q f) -> (e q) f", f=BW - B1W)).then_inc(fb_in, 16)
                sp.wait_ge(zero_ready, 1)
                sp.dma_start(sorted_x.rearrange("(j p) c -> p j c", p=P),
                             T["zeros"][:].unsqueeze(1).broadcast_to([P, NR, C])).then_inc(zero_out, 16)
                for g in range(NG):
                    place(0, g)
                sp.wait_ge(wsplit_low, 4)
                sp.wait_ge(lg_done, 1)
                sp.dma_start(w1_sb[:].rearrange("p (e f) -> p e f", e=E), w1.rearrange("e c f -> c e f")).then_inc(f_in, 16)
                for k in range(FB):
                    sp.dma_start(w2_sb[:, k], w2.rearrange("e (k p) c -> k p e c", p=P)[k]).then_inc(f_in, 16)
                sp.wait_ge(bias_split, 1)
                for i in range(3):
                    sp.dma_start(b1_sb[i:i + 1, :].rearrange("a (p f) -> a p f", f=B1W),
                                 T["bias_parts"][:, i, 0:B1W]).then_inc(fb_spread, 16)
                    sp.dma_start(b2_sb[i:i + 1, :].rearrange("a (p f) -> a p f", p=P),
                                 T["bias_parts"][:, i, B1W:BW]).then_inc(fb_spread, 16)

            def store(b):
                ov = out.rearrange("b (n p) c -> b p n c", p=P)[bass.ds(b, 1)].rearrange("a p n c -> (a p) n c")
                sp.dma_start(ov, res[:]).then_inc(out_done, 16)

            def body(b, last):
                if not at(b, 0):
                    place(b, NG - 1)
                if not at(b, 0, 1):
                    sp.wait_ge(res_ready, b - 1)
                    sp.sem_inc(store_turn, 1)
                    store(b - 1)
                if not last:
                    for g in range(NG - 1):
                        place(b + 1, g)
                else:
                    sp.wait_ge(res_ready, B - 1)
                    store(0)

            def finish(b):
                if b == B - 1:
                    sp.wait_ge(res_ready, B)
                    store(b)

            def experts():
                sp.wait_ge(scattered, 16 * NT)


                def load(t, i):
                    wait(sp, xsT_done, t - 1)
                    sp.dma_start(xs[:, i, :], sorted_x[bass.ds(t * P, P), :]).then_inc(xs_in[i], 16)
                load(0, 0)
                load(1, 1)
                with sp.Fori(1, NR // 2) as m:
                    for i in range(2):
                        load(2 * m + i, i)
                for q in range(2):
                    n = slice(q * NR // 2, (q + 1) * NR // 2)
                    sp.wait_ge(g_ready, q + 1)
                    sp.dma_start(sorted_g.rearrange("(j p) c -> p j c", p=P)[:, n, :], z[:, n, :]).then_inc(g_out, 16)

            program(sp, start, body, finish, experts)
            sp.wait_ge(out_done, 16 * B + 16)

        @block.gpsimd
        def _(pool):
            def rotated(b, n):
                pool.wait_ge(rope_done, NI * b + n + 1)
                g = n // 2
                if g >= 2:
                    pool.wait_ge(qk_in[g - 2], 128 * b + 128)
                else:
                    wait(pool, qk_in[g + 2], 128 * b)
                pool.tensor_tensor(staged[:, g % 2, :, n % 2, :], rot_out[:, n % 2, :, 0:S], rot_out[:, n % 2, :, S:2 * S],
                                   op=ALU.add).then_inc(staged_ready, 1)

            def scale(b, h):
                pool.wait_ge(rden_ready, H * b + h + 1)
                wait(pool, probsT_done, H * b + h - 1)
                pool.sem_inc(scale_turn, 1)
                for i, c in enumerate(rows):
                    m = pool.tensor_scalar(probs[:, h % 2, c], pexp[:, h % 4, c], rden[:, h % 4, i:i + 1], 1.0,
                                           ALU.mult, ALU.mult)
                m.then_inc(probs_ready, 1)

            def scatter(n):
                if n == 0:
                    pool.wait_ge(zero_out, 16)
                    pool.wait_ge(pos_ready, 1)
                pool.indirect_dma_start(
                    out=sorted_x, out_offset=bass.IndirectOffsetOnAxis(ap=pos[:, n:n + 1], axis=0),
                    in_=xn[:, n, :], in_offset=None).then_inc(scattered, 16)

            def gather(n):
                if n == 0:
                    pool.wait_ge(scattered, 16 * NT)
                    pool.wait_ge(g_out, 32)
                pool.indirect_dma_start(
                    out=gate[:, n, :], out_offset=None, in_=sorted_g,
                    in_offset=bass.IndirectOffsetOnAxis(ap=pos[:, n:n + 1], axis=0)).then_inc(g_in, 16)

            def start():
                pool.memset(T["zeros"][:], 0.0).then_inc(zero_ready, 1)
                pool.memset(mask[:, P:2 * P], 0.0)
                pool.memset(lat[:].bitcast(F32), 0.0)
                pool.memset(T["halfneg"][:], -0.5).then_inc(zero_ready, 1)
                pool.wait_ge(zero_ready, 2)
                def rstd(q):
                    n = slice(q * NT // 4, (q + 1) * NT // 4)
                    pool.wait_ge(var_ready, q + 1)
                    pool.tensor_tensor(T["rstd"][:, n], T["veps"][:, n], T["halfneg"][:, n],
                                       op=ALU.pow).then_inc(rstd_ready, 1)
                rstd(0)
                rstd(1)
                for n in range(NI):
                    if n in (2, 4):
                        rstd(n // 2 + 1)
                    rotated(0, n)
                scale(0, 0)

            def body(b, last):
                for h in range(H):
                    if not (last and h == H - 1) and by_pool(*after(b, h)):
                        scale(*after(b, h))
                    if h == 1 and not at(b, 0):
                        rotated(b, NI - 1)
                    if h % 2 and h > 1 and not last:
                        rotated(b + 1, (h - 3) // 2)
                    if at(b, 0, 1) and h >= 4:
                        for n in ((2 * h - 8, 2 * h - 7) if h < 8 else (h,)):
                            (scatter, gather)[b](n)

            program(pool, start, body, lambda b: None, lambda: None)

        @block.vector
        def _(dve):
            step = [0]

            def then(ins):
                step[0] += 1
                ins.then_inc(dve_step, 1)
                dve.wait_ge(dve_step, step[0])

            def rotate(b, n, r):
                if r == 0:
                    dve.wait_ge(proj_done, NI * b + n + 1)
                    wait(dve, staged_ready, NI * b + n - 1)
                m = dve.tensor_tensor(rot_out[:, n % 2, r, :], j_bank[n % 2][:], rot[:, r, :], op=ALU.mult)
                if r == 1:
                    m.then_inc(rope_done, 1)

            def row_max(b, h):
                for i, c in enumerate(rows):
                    t = dve.tensor_tensor_reduce(masked[:, h % 2, c], s_bank[h % 2][:, c], mask[:, c], -1.0, -NEG * 1e8,
                                                 ALU.add, ALU.min, negmax[:, h % 2, i:i + 1])
                t.then_inc(masked_ready, 1)

            def denominators(b, h, ahead=True):
                dve.wait_ge(exp_done, H * b + h + 1)
                if ahead:
                    dve.wait_ge(scores_done, H * b + h + 3)
                dve.reciprocal(rden[:, h % 4, :], rowsum[:, h % 4, :]).then_inc(rden_ready, 1)

            def scale(b, h):
                if at(b, 0) and h == POOL_HEADS:
                    dve.wait_ge(probs_ready, h)
                dve.wait_ge(rden_ready, H * b + h + 1)
                wait(dve, probsT_done, H * b + h - 1)
                for i, c in enumerate(rows):
                    m = dve.tensor_scalar(probs[:, h % 2, c], pexp[:, h % 4, c], rden[:, h % 4, i:i + 1], None, ALU.mult)
                m.then_inc(probs_ready, 1)

            def probs_low(b, h):
                dve.wait_ge(probsT_high, H * b + h + 1)
                dve.tensor_tensor(probsT[:, h % 2, 1, :], t_bank[h % 2][:, 0:SW], probsT[:, h % 2, 0, :].bitcast(F32),
                                  op=ALU.subtract).then_inc(probsT_ready, 1)

            def stats(q):
                dve.wait_ge(x_in[q], 16)
                n4 = range(q * NT // 4, (q + 1) * NT // 4)
                for n in n4:
                    last = dve.bn_stats(T["st6"][:, n, :], x_sb[:, n, :])
                then(last)
                for n in n4:
                    last = dve.bn_aggr(T["mv"][:, n, :], T["st6"][:, n, :])
                then(last)
                n = slice(q * NT // 4, (q + 1) * NT // 4)
                dve.tensor_scalar(T["veps"][:, n], T["mv"][:, n, 1], LN_EPS, None, ALU.add).then_inc(var_ready, 1)

            def normalise(q):
                dve.wait_ge(rstd_ready, q + 1)
                for n in range(q * NT // 4, (q + 1) * NT // 4):
                    dve.tensor_scalar(xn[:, n, :], x_sb[:, n, :], T["mv"][:, n, 0:1], T["rstd"][:, n:n + 1],
                                      ALU.subtract, ALU.mult).then_inc(xn_ready, 1)

            def turned_low(q):
                dve.wait_ge(xT_high, q + 1)
                c = slice(q * 512, (q + 1) * 512)
                dve.tensor_tensor(xnT_l[:, c], bank[q][:], xnT_h[:, c].bitcast(F32), op=ALU.subtract).then_inc(xT_low, 1)

            def route_top():
                hot, top, topi = T["hot"], T["top"], T["topi"]
                dve.wait_ge(lg_done, 1)
                then(dve.tensor_tensor(T["lg"][:], y_bank[:, 0:NT * E].rearrange("p (n e) -> p n e", e=E),
                                       T["gb"][:].unsqueeze(1).broadcast_to([P, NT, E]), op=ALU.add))
                for n in range(NT):
                    last = dve.max(top[:, n, :], T["lg"][:, n, :])
                then(last)

            def route_index():
                hot, top, topi = T["hot"], T["top"], T["topi"]
                for n in range(NT):
                    last = dve.max_index(topi[:, n, :], top[:, n, :], T["lg"][:, n, :])
                then(last)
                then(dve.tensor_copy(T["topf"][:], topi[:, :, 0:2]))
                then(dve.tensor_reduce(T["estar"][:], T["topf"][:], X_AXIS, ALU.max))
                then(dve.tensor_tensor(hot[:], T["cex"][:], T["estar"][:].unsqueeze(2).broadcast_to([P, NT, E]),
                                       op=ALU.is_equal))
                dve.tensor_copy(T["hot16"][:], hot[:]).then_inc(hot_ready, 1)

            def route_place():
                dve.wait_ge(cnt_done, 1)
                then(dve.tensor_scalar(T["cnt_i"][:], y_bank[:, 256:256 + E], float(P - 1), None, ALU.add))
                then(dve.tensor_scalar(T["tiles_i"][:], T["cnt_i"][:], 7, None, ALU.arith_shift_right))
                then(dve.tensor_copy(T["tiles_f"][:], T["tiles_i"][:]))
                tb = T["tiles_f"][:].unsqueeze(1).broadcast_to([P, E, E])
                prod, base, rank = T["prod"], T["base"], T["rank"]
                dve.tensor_tensor(prod[:, 0], T["cexcl"][:], tb, op=ALU.mult)
                then(dve.tensor_tensor(prod[:, 1], T["cincl"][:], tb, op=ALU.mult))
                dve.tensor_reduce(T["excl"][:], prod[:, 0], X_AXIS, ALU.add)
                then(dve.tensor_reduce(T["incl"][:], prod[:, 1], X_AXIS, ALU.add))
                then(dve.tensor_scalar(base[:], T["excl"][:], float(P), None, ALU.mult))
                then(dve.tensor_tensor(rank[:], y_bank[:, 0:NT * E].rearrange("p (n e) -> p n e", e=E),
                                       base[:].unsqueeze(1).broadcast_to([P, NT, E]), op=ALU.add))
                then(dve.tensor_tensor(T["rank2"][:], rank[:], T["hot"][:], op=ALU.mult))
                then(dve.tensor_reduce(T["posf"][:], T["rank2"][:], X_AXIS, ALU.add))
                dve.tensor_copy(pos[:], T["posf"][:]).then_inc(pos_ready, 1)
                then(dve.tensor_tensor(T["cmp"][:], T["incl"][0:1, :].unsqueeze(1).broadcast_to([1, NR, E]),
                                       T["ctile"][:], op=ALU.is_le))
                then(dve.tensor_reduce(T["tef"][:], T["cmp"][:], X_AXIS, ALU.add))
                dve.tensor_scalar(tile_e[:], T["tef"][:], float(E - 1), None, ALU.min).then_inc(tile_ready, 1)

            def split_biases():
                parts, rest = T["bias_parts"], T["bias_rest"]
                dve.wait_ge(fb_in, 32)
                then(dve.tensor_copy(parts[:, 0, :], T["bias_in"][:]))
                then(dve.tensor_tensor(rest[:, 0, :], T["bias_in"][:], parts[:, 0, :], op=ALU.subtract))
                then(dve.tensor_copy(parts[:, 1, :], rest[:, 0, :]))
                then(dve.tensor_tensor(rest[:, 1, :], rest[:, 0, :], parts[:, 1, :], op=ALU.subtract))
                dve.tensor_copy(parts[:, 2, :], rest[:, 1, :]).then_inc(bias_split, 1)

            def start():
                def weight_low(n, lo, hi, whole, k):
                    dve.wait_ge(wsplit_high, n + 1)
                    dve.scalar_tensor_tensor(out=lo, in0=whole, scalar=k, in1=hi.bitcast(F32), op0=ALU.mult,
                                             op1=ALU.subtract).then_inc(wsplit_low, 1)

                def latents_low(q):
                    dve.wait_ge(latT_high, q + 1)
                    c = slice(q * 512, (q + 1) * 512)
                    dve.tensor_tensor(latT[LAT:P, c], bank[6][LAT:P, :], latT[LAT:P, c].bitcast(F32),
                                      op=ALU.subtract).then_inc(latT_low, 1)

                dve.memset(ones16[:], 1.0).then_inc(hot_ready, 1)
                stats(0)
                normalise(0)
                weight_low(0, T["wdnT_l"][:], T["wdnT_h"][:], T["wdnT"][:], 1.0)
                weight_low(1, T["gw_l"][:], T["gw_h"][:], T["gw"][:], 1.0)
                turned_low(0)
                weight_low(2, wq_l[:], wq_h[:], T["wq_in"][:], HD ** -0.5)
                weight_low(3, wk_l[:], wk_h[:], T["wkup"][:], 1.0)
                latents_low(0)
                stats(1)
                dve.wait_ge(m_in, 48)
                for n in range(NI):
                    rotate(0, n, 0)
                    rotate(0, n, 1)
                    q = n // 2
                    if n in (0, 2, 4):
                        normalise(q + 1)
                    if n in (1, 3):
                        stats(q + 2)
                    if n in (2, 4, 6):
                        turned_low(q)
                    if n in (3, 5, 7):
                        latents_low(q)
                dve.wait_ge(zero_ready, 2)
                for h in range(3):
                    dve.wait_ge(scores_done, h + 1)
                    if h == 2:
                        dve.wait_ge(exp_done, 1)
                    row_max(0, h)
                dve.wait_ge(c_in, 16 * NC_IN)
                dve.tensor_copy(T["cbef16"][:], T["cbef"][:]).then_inc(hot_ready, 1)
                denominators(0, 0, ahead=False)

            def latents(b):
                if at(b, 0):
                    dve.wait_ge(lat_copied, 1)
                wait(dve, pv_done, H * b)
                dve.tensor_copy(lat[:, :, :, LAT:2 * LAT], lat_all[:, bass.ds(2 * b, 2), :, :].bitcast(F32)
                                .rearrange("p n s l -> p s n l")).then_inc(lat_ready, 1)

            def gate_product(b):
                dve.wait_ge(y_done, b + 1)
                dve.wait_ge(g_in, 16 * NT)
                dve.wait_ge(out_done, 16 * b)
                dve.tensor_tensor(gated[:].rearrange("p n c -> p (n c)"), y_bank[:, 0:2 * C],
                                  gate[:, bass.ds(2 * b, 2), :].rearrange("p n c -> p (n c)"),
                                  op=ALU.mult).then_inc(y_read, 1)

            def residual(b):
                dve.wait_ge(y_read, b + 1)
                dve.tensor_tensor(res[:], gated[:], x_sb[:, bass.ds(2 * b, 2), :], op=ALU.add).then_inc(res_ready, 1)

            def body(b, last):
                for h in range(H):
                    if not (last and h == H - 1):
                        denominators(*after(b, h), ahead=(h + 3 < H or not last))
                    if h + 3 < H:
                        row_max(b, h + 3)
                    elif not last:
                        row_max(b + 1, h + 3 - H)
                    if not last and not by_pool(*after(b, h)):
                        scale(*after(b, h))
                    probs_low(b, h)
                    if h == 0:
                        latents(b)
                        if not at(b, 0, 1):
                            rotate(b, NI - 1, 1)
                    elif not last:
                        if h % 2:
                            rotate(b + 1, h // 2, 0)
                        else:
                            rotate(b + 1, h // 2 - 1, 1)
                    if h == 2 and not at(b, 0, 1):
                        gate_product(b - 1)
                    if h == 3 and not at(b, 0, 1):
                        residual(b - 1)
                    if at(b, 0) and h < 4:
                        (route_top, route_index, split_biases, route_place)[h]()
                    if last and h == 8:
                        dve.wait_ge(out_done, 16 * (B - 1))
                        then(dve.tensor_tensor(y_keep[:], y_keep[:], gate[:, 0:2, :], op=ALU.mult))
                        dve.tensor_tensor(res[:], y_keep[:], x_sb[:, 0:2, :], op=ALU.add).then_inc(res_ready, 1)

            def finish(b):
                if b == 0:
                    rotate(1, NI - 1, 1)
                    dve.wait_ge(y_done, 1)
                    dve.tensor_copy(y_keep[:].rearrange("p n c -> p (n c)"), y_bank[:, 0:2 * C]).then_inc(y_read, 1)
                else:
                    dve.wait_ge(out_done, 16 * B)
                    gate_product(b)
                    residual(b)

            def experts():
                def step(t, i):
                    o = 1 - i
                    if has(t, 2):
                        dve.wait_ge(xsT_done, t + 3)
                        wait(dve, h_done, t + 1)
                        dve.tensor_copy(xsT[:, i, :], bank[i][:, 0:P]).then_inc(xsT_ready, 1)
                    if has(t, 0):
                        dve.wait_ge(hidT_done, t + 1)
                        wait(dve, e_done, t - 1)
                        dve.tensor_copy(hidT[:, i].rearrange("p k n -> p (k n)"), t_bank[i][:]).then_inc(hidT_ready, 1)
                    if has(t, -1):
                        dve.wait_ge(e_done, t)
                        dve.tensor_scalar(z[:, bass.ds(t - 1, 1), :].rearrange("p a c -> p (a c)"), bank[6 + o][:, 0:C],
                                          float(TOP_K), None, ALU.mult).then_inc(z_ready, 1)
                dve.wait_ge(xsT_done, 1)
                dve.tensor_copy(xsT[:, 0, :], bank[0][:, 0:P]).then_inc(xsT_ready, 1)
                over_tiles(dve, step)

            program(dve, start, body, finish, experts)

        @block.scalar
        def _(act):
            def exponentials(b, h):
                act.wait_ge(masked_ready, H * b + h + 1)
                wait(act, probs_ready, H * b + h - 3)
                for i, c in enumerate(rows):
                    e = act.activation(pexp[:, h % 4, c], masked[:, h % 2, c], ACT.Exp, bias=negmax[:, h % 2, i:i + 1],
                                       scale=-1.0, accum_out=rowsum[:, h % 4, i:i + 1])
                e.then_inc(exp_done, 1)

            def probs_high(b, h):
                act.wait_ge(probsT_done, H * b + h + 1)
                wait(act, pv_done, H * b + h - 1)
                act.copy(probsT[:, h % 2, 0, :], t_bank[h % 2][:, 0:SW]).then_inc(probsT_high, 1)

            def ctx_out(b, p):
                act.wait_ge(pv_done, H * b + 2 * p + 2)
                if p == 0:
                    wait(act, y_done, b)
                act.copy(ctxT[:, p, :], o_bank[:, 0:S]).then_inc(ctx_ready, 1)

            def start():
                act.wait_ge(wd_in, 32)
                act.copy(T["wdnT_h"][:], T["wdnT"][:]).then_inc(wsplit_high, 1)
                act.copy(T["gw_h"][:], T["gw"][:]).then_inc(wsplit_high, 1)

                def latents_copied(q):
                    act.wait_ge(lat_turned, q + 1)
                    act.copy(lat_all[:, q * NT // 4:(q + 1) * NT // 4].rearrange("p n s l -> p (n s l)"),
                             bank[7][:]).then_inc(lat_copied, 1)

                for q in range(4):
                    c = slice(q * 512, (q + 1) * 512)
                    act.wait_ge(xT_done, q + 1)
                    act.copy(xnT_h[:, c], bank[q][:]).then_inc(xT_high, 1)
                    if q == 0:
                        act.wait_ge(wq_in, 16)
                        act.mul(wq_h[:], T["wq_in"][:], HD ** -0.5).then_inc(wsplit_high, 1)
                    if q == 1:
                        act.wait_ge(vo_done, 1)
                        for i in range(2):
                            act.copy(vo_sb[:, 4 * i:4 * i + 4, :].rearrange("p n c -> p (n c)"), bank[2 + i][:]).then_inc(vo_ready, 1)
                    act.wait_ge(latT_done, q + 1)
                    act.copy(latT[:, c], bank[6][:]).then_inc(latT_high, 1)
                    if q == 0:
                        act.wait_ge(wk_in, 16)
                        act.copy(wk_h[:], T["wkup"][:]).then_inc(wsplit_high, 1)
                    act.wait_ge(lgT_done, q + 1)
                    act.copy(T["lgT"][:, c], bank[q][0:E, :]).then_inc(lgT_ready, 1)
                    if q > 0:
                        latents_copied(q - 1)
                latents_copied(3)
                for h in range(2):
                    exponentials(0, h)

            def body(b, last):
                for h in range(H):
                    if h + 2 < H:
                        exponentials(b, h + 2)
                    elif not last:
                        exponentials(b + 1, h + 2 - H)
                    probs_high(b, h)
                    if h == 0 and not at(b, 0, 1):
                        ctx_out(b - 1, NP - 1)
                    if h % 2 == 0 and h > 0:
                        ctx_out(b, h // 2 - 1)

            def finish(b):
                ctx_out(b, NP - 1)

            def experts():
                def step(t, i):
                    if has(t, 1):
                        act.wait_ge(h_done, t + 2)
                        wait(act, hidT_done, t)
                        act.activation(hid[:, 1 - i, :], j_bank[1 - i][:], ACT.Gelu).then_inc(hid_ready, 1)
                over_tiles(act, step)
                for q in range(2):
                    n = slice(q * NR // 2, (q + 1) * NR // 2)
                    act.wait_ge(z_ready, (q + 1) * NR // 2)
                    act.activation(z[:, n, :], z[:, n, :], ACT.Silu).then_inc(g_ready, 1)

            program(act, start, body, finish, experts)

        @block.tensor
        def _(pe):
            def split_matmul(o, lhs, rhs, start=True, stop=True):
                (lh, ll), (rh, rl) = lhs, rhs
                pe.matmul(o, lh, rh, start=start, stop=False)
                pe.matmul(o, lh, rl, start=False, stop=False)
                return pe.matmul(o, ll, rh, start=False, stop=stop)

            def project(b, n):
                g = n // 2
                wait(pe, rope_done, NI * b + n - 1)
                for half in range(2):
                    c = slice((2 * g + half) * P, (2 * g + half + 1) * P)
                    o, t = j_bank[n % 2][:, half * S:(half + 1) * S], bass.ds(b * S, S)
                    if n % 2 == 0:
                        m = split_matmul(o, (wq_h[:, c], wq_l[:, c]), (xnT_h[:, t], xnT_l[:, t]))
                    else:
                        pe.matmul(o, wk_h[:, c], latT[:, t], start=True, stop=False)
                        m = pe.matmul(o, wk_l[:, c], latT[:, t], start=False, stop=True)
                m.then_inc(proj_done, 1)

            def scores(b, h):
                r, p = slice(HD * (h % 2), HD * (h % 2) + HD), h // 2
                if h % HPG == 0:
                    pe.wait_ge(qk_in[h // HPG], 128 * b + 128)
                wait(pe, masked_ready, H * b + h - 1)
                pe.matmul(s_bank[h % 2][:, 0:P], qk_sb[r, 0, p, 0:P], qk_sb[r, 1, p, 0:P], start=True, stop=True)
                pe.matmul(s_bank[h % 2][:, P:SW], qk_sb[r, 0, p, P:S], qk_sb[r, 1, p, :],
                          start=True, stop=True).then_inc(scores_done, 1)

            def turn(b, h):
                pe.wait_ge(probs_ready, H * b + h + 1)
                wait(pe, probsT_ready, H * b + h - 1)
                for k in range(3):
                    t = pe.transpose(t_bank[h % 2][:, k * P:(k + 1) * P], probs[:, h % 2, k * P:(k + 1) * P], ident[:])
                t.then_inc(probsT_done, 1)

            def values(b, h):
                if h == 0:
                    pe.wait_ge(lat_ready, b + 1)
                if h % 2 == 0:
                    wait(pe, ctx_ready, NP * b + h // 2)
                pe.wait_ge(probsT_ready, H * b + h + 1)
                c = slice(LAT, 3 * LAT) if h % 2 == 0 else slice(0, 2 * LAT)
                split_matmul(o_bank[:, 0:S], [lat[:, k, 0, c] for k in range(2)],
                             [probsT[:, h % 2, k, 0:S] for k in range(2)], start=(h % 2 == 0), stop=False)
                split_matmul(o_bank[:, P:S], [lat[:, k, 1, c] for k in range(2)],
                             [probsT[:, h % 2, k, S:SW] for k in range(2)], start=False,
                             stop=(h % 2 == 1)).then_inc(pv_done, 1)

            def output(b, p):
                if p == 0:
                    wait(pe, y_read, b)
                pe.wait_ge(ctx_ready, NP * b + p + 1)
                for i in range(2):
                    m = pe.matmul(y_bank[:, i * C:(i + 1) * C], ctxT[:, p, i * P:(i + 1) * P], vo_sb[:, p, :],
                                  start=(p == 0 and i == 0), stop=(p == NP - 1), skip_group_check=True)
                if p == NP - 1:
                    m.then_inc(y_done, 1)

            def turn_rows(q):
                for n in range(q * NT // 4, (q + 1) * NT // 4):
                    pe.wait_ge(xn_ready, n + 1)
                    t = pe.transpose(bank[q][:, (n % 4) * P:(n % 4 + 1) * P], xn[:, n, :], ident[:])
                t.then_inc(xT_done, 1)

            def count_tokens():
                hot16 = T["hot16"]
                pe.wait_ge(hot_ready, 3)
                pe.matmul(y_bank[:, 0:NT * E], T["cbef16"][:], hot16[:].rearrange("p n e -> p (n e)"),
                          start=True, stop=False, skip_group_check=True)
                for n in range(NT - 1):
                    pe.matmul(y_bank[:, (n + 1) * E:NT * E].rearrange("p (n e) -> p n e", e=E), ones16[:],
                              hot16[:, n:n + 1, :].broadcast_to([P, NT - 1 - n, E]),
                              start=False, stop=(n == NT - 2), skip_group_check=True)
                for n in range(NT):
                    m = pe.matmul(y_bank[:, 256:256 + E], ones16[:], hot16[:, n, :], start=False, stop=(n == NT - 1),
                                  skip_group_check=True)
                m.then_inc(cnt_done, 1)

            def start():
                def latents_of(q):
                    c = slice(q * 512, (q + 1) * 512)
                    if q == 0:
                        pe.wait_ge(wsplit_low, 2)
                    pe.wait_ge(xT_low, q + 1)
                    wait(pe, latT_low, q)
                    split_matmul(bank[6][:], (T["wdnT_h"][:], T["wdnT_l"][:]), (xnT_h[:, c], xnT_l[:, c])).then_inc(latT_done, 1)
                    split_matmul(bank[q][0:E, :], (T["gw_h"][:], T["gw_l"][:]), (xnT_h[:, c], xnT_l[:, c])).then_inc(lgT_done, 1)

                def turn_latents(q):
                    pe.wait_ge(latT_low, q + 1)
                    wait(pe, lat_copied, q)
                    for n in range(4):
                        k = (4 * q + n) * P
                        m = pe.transpose(bank[7][:, n * P:(n + 1) * P], latT[:, k:k + P].bitcast(F32), ident[:])
                    m.then_inc(lat_turned, 1)

                pe.wait_ge(id_in, 16)
                for q in range(4):
                    if q == 2:
                        pe.wait_ge(vo_ready, 2)
                    turn_rows(q)
                    if q == 0:
                        latents_of(0)
                        pe.wait_ge(wsplit_low, 3)
                        project(0, 0)
                        pe.wait_ge(wsplit_low, 4)
                        pe.wait_ge(latT_low, 1)
                        project(0, 1)
                        continue
                    for n in (2 * q, 2 * q + 1):
                        project(0, n)
                    if q == 1:
                        pe.wait_ge(w_in, 32)
                        for h in range(H):
                            r = slice(HD * (h % 2), HD * (h % 2) + HD)
                            m = pe.matmul(bank[2 + h // 8][r, (h // 2 % 4) * C:(h // 2 % 4 + 1) * C], T["wv_sb"][r, h // 2, :],
                                          T["wo_sb"][r, h // 2, :], start=True, stop=True)
                        m.then_inc(vo_done, 1)
                    latents_of(q)
                    turn_latents(q - 1)
                turn_latents(3)
                pe.wait_ge(lat_copied, 4)
                pe.wait_ge(lgT_ready, 4)
                for n in range(NT):
                    m = pe.transpose(y_bank[:, n * E:(n + 1) * E], T["lgT"][:, n * P:(n + 1) * P], ident[0:E, 0:E])
                m.then_inc(lg_done, 1)
                for h in range(3):
                    scores(0, h)

            def body(b, last):
                for h in range(H):
                    if h + 3 < H:
                        scores(b, h + 3)
                    elif not last:
                        scores(b + 1, h + 3 - H)
                    turn(b, h)
                    if h > 0:
                        values(b, h - 1)
                    elif not at(b, 0, 1):
                        values(b - 1, H - 1)
                    if at(b, 0) and h == 2:
                        count_tokens()
                    if at(b, 0) and h == 7:
                        pe.wait_ge(pos_ready, 1)
                        for p in range(3):
                            output(b, p)
                    elif h == 1 and not at(b, 0, 1):
                        output(b - 1, NP - 1)
                    elif h % 2 and h >= (9 if at(b, 0) else 3):
                        output(b, h // 2 - 1)
                    if h % 2 == 0 and not last:
                        project(b + 1, h // 2)

            def finish(b):
                values(b, H - 1)
                output(b, NP - 1)

            def experts():
                pe.wait_ge(fb_spread, 96)
                pe.wait_ge(f_in, 16 * (1 + FB))
                pe.wait_ge(tile_ready, 1)
                pe.wait_ge(masked_ready, H + 3)
                pe.wait_ge(rope_done, 2 * NI)
                pe.wait_ge(y_read, 1)

                def experts_of(first, count):
                    return nc.values_load_multi_w_load_instructions(
                        tile_e[0:1, bass.ds(first, count)], engines=[mybir.EngineType.PE], min_val=0, max_val=E - 1)[1]

                ids = [None] * 4

                def turn_tile(t, i):
                    pe.wait_ge(xs_in[i], (t - i) * 8 + 16)
                    wait(pe, xsT_ready, t - 1)
                    pe.transpose(bank[i][:, 0:P], xs[:, i, :], ident[:]).then_inc(xsT_done, 1)

                def step(t, i):
                    o = 1 - i
                    if i == 0 or at(t, -1):
                        lo, hi = (0, 4) if not isinstance(t, int) else (max(0, i + 1 - t), min(4, i + NR - t))
                        ids[lo:hi] = experts_of(t - i + lo - 1, hi - lo)
                    if has(t, 1):
                        e = ids[2 + i]
                        pe.wait_ge(xsT_ready, t + 2)
                        wait(pe, hid_ready, t)
                        pe.matmul(j_bank[o][:], ones16[0:3, :], b1_sb[:, bass.ds(e * FF, FF)], start=True, stop=False)
                        pe.matmul(j_bank[o][:], xsT[:, o, :], w1_sb[:, bass.ds(e * FF, FF)],
                                  start=False, stop=True).then_inc(h_done, 1)
                    if has(t, 2):
                        turn_tile(t + 2, i)
                    if has(t, 0):
                        pe.wait_ge(hid_ready, t + 1)
                        wait(pe, hidT_ready, t - 1)
                        for k in range(FB):
                            m = pe.transpose(t_bank[i][:, k * P:(k + 1) * P], hid[:, i, k * P:(k + 1) * P], ident[:])
                        m.then_inc(hidT_done, 1)
                    if has(t, -1):
                        e = ids[i]
                        pe.wait_ge(hidT_ready, t)
                        wait(pe, z_ready, t - 2)
                        pe.matmul(bank[6 + o][:, 0:C], ones16[0:3, :], b2_sb[:, bass.ds(e * C, C)], start=True, stop=False)
                        for k in range(FB):
                            m = pe.matmul(bank[6 + o][:, 0:C], hidT[:, o, k, :],
                                          w2_sb[:, k, :, :].rearrange("p e c -> p (e c)")[:, bass.ds(e * C, C)],
                                          start=False, stop=(k == FB - 1))
                        m.then_inc(e_done, 1)
                turn_tile(0, 0)
                over_tiles(pe, step)
                pe.wait_ge(z_ready, NR)

            program(pe, start, body, finish, experts)


def kernel(**inputs):
    import concourse.bacc as bacc
    from concourse.bass_utils import run_bass_kernel_spmd

    g = {k: np.asarray(v) for k, v in inputs.items()}
    by_half = lambda w: w.reshape(NG, HPG, 2, HALF, -1).transpose(4, 0, 2, 1, 3).reshape(w.shape[1], H * HD)
    arrays = {
        "x": g["L0_attn_x"],
        "wqT": by_half(g["L0_attn_wq"]),
        "w_downT": np.tile(g["L0_attn_w_kv_down"].T, (1, 2)),
        "w_kupT": np.tile(by_half(g["L0_attn_w_k_up"]), (2, 1)),
        "w_vup": g["L0_attn_w_v_up"].reshape(NP, 2 * HD, LAT).transpose(1, 0, 2),
        "woT": g["L0_attn_wo"].reshape(C, NP, 2 * HD).transpose(2, 1, 0),
        "gate_w": g["L0_ffn_gate_w"],
        "gate_b": g["L0_ffn_gate_b"],
        "w1": g["L0_ffn_w1"],
        "b1": g["L0_ffn_b1"],
        "w2": g["L0_ffn_w2"],
        "b2": g["L0_ffn_b2"],
        **host_constants(),
    }
    arrays = {k: np.ascontiguousarray(v) for k, v in arrays.items()}
    nc = bacc.Bacc("TRN2", target_bir_lowering=False, num_devices=1)
    aps = {k: nc.dram_tensor(f"in_{k}", v.shape, mybir.dt.from_np(v.dtype), kind="ExternalInput").ap()
           for k, v in arrays.items()}
    out = nc.dram_tensor("out", (B, S, C), F32, kind="ExternalOutput").ap()
    build(nc, **aps, out=out)
    r = run_bass_kernel_spmd(nc, [{f"in_{k}": v for k, v in arrays.items()}], core_ids=[0])
    return r.results[0]["out"]
```

```python
from contextlib import ExitStack

import numpy as np

import concourse.bass as bass
from concourse import mybir

F32 = mybir.dt.float32
F32R = mybir.dt.float32r
BF16 = mybir.dt.bfloat16
I32 = mybir.dt.int32
U32 = mybir.dt.uint32
ALU = mybir.AluOpType
ACT = mybir.ActivationFunctionType
X_AXIS = mybir.AxisListType.X

P = 128
B, S, C = 8, 256, 128
NT = B * S // P
TPB = S // P
H, HD = 16, 64
HALF = HD // 2
LAT = 64
NG = 4
HPG = H // NG
NP = H // 2
NI = 2 * NG
E, FF = 8, 512
FB = FF // P
TOP_K = 2
NR = NT + E - 2
FW = FF + FB
BW = E * C // P
LN_EPS = 1e-5
NEG = -1e30
SW = P + S


def host_constants():
    f = np.float32
    inv = (f(1.0) / f(10000.0) ** (np.arange(0, HD, 2, dtype=f) / f(HD))).astype(f)
    ang = np.arange(S, dtype=f)[None, :] * np.tile(inv, HPG)[:, None]
    cos, sin = np.cos(ang).astype(f), np.sin(ang).astype(f)
    k = np.arange(P)
    e = np.arange(E, dtype=f)
    return {
        "c_rot": np.stack([np.concatenate([cos, -sin], 1), np.concatenate([sin, cos], 1)], 1).astype(f),
        "c_ident": np.eye(P, dtype=f),
        "c_mask": np.where(k[None, :] > k[:, None], f(NEG), f(0.0)).astype(f),
        "c_before": (k[:, None] < k[None, :]).astype(f),
        "c_expert": np.broadcast_to(e, (P, NT, E)).astype(f),
        "c_excl": np.broadcast_to((e[None, :] < e[:, None]).astype(f), (P, E, E)).copy(),
        "c_incl": np.broadcast_to((e[None, :] <= e[:, None]).astype(f), (P, E, E)).copy(),
        "c_tile": np.broadcast_to(np.arange(NR, dtype=f)[:, None], (P, NR, E)).copy(),
    }


def wait(eng, s, v):
    if not isinstance(v, int) or v > 0:
        eng.wait_ge(s, v)


def build(nc, x, wqT, w_downT, w_kupT, w_vup, woT, gate_w, gate_b, w1, b1, w2, b2,
          c_rot, c_ident, c_mask, c_before, c_expert, c_excl, c_incl, c_tile, out):
    with ExitStack() as ctx:
        def sb(name, shape, dt=F32):
            return ctx.enter_context(nc.sbuf_tensor(name, shape, dt))

        def sem(name):
            return ctx.enter_context(nc.semaphore(name))

        bank = [ctx.enter_context(nc.psum_tensor(f"bank{i}", [P, 512], F32)) for i in range(8)]
        s_bank, t_bank, j_bank, o_bank, y_bank = bank[0:2], bank[2:4], bank[4:6], bank[6], bank[7]

        sorted_x = nc.dram_tensor("sorted_x", [NR * P, C], F32).ap()
        sorted_g = nc.dram_tensor("sorted_g", [NR * P, C], F32).ap()

        ident = sb("ident", [P, P])
        mask = sb("mask", [P, SW])
        x_sb = sb("x_sb", [P, NT, C])
        xn = sb("xn", [P, NT, C])
        gate = xn
        xnT_h = sb("xnT_h", [P, NT * P], F32R)
        xnT_l = sb("xnT_l", [P, NT * P], F32R)
        rot = sb("rot", [P, 2, 2 * S])
        wq_h = sb("wq_h", [P, H * HD], F32R)
        wq_l = sb("wq_l", [P, H * HD], F32R)
        wk_h = sb("wk_h", [P, H * HD], F32R)
        wk_l = sb("wk_l", [P, H * HD], F32R)
        vo_sb = sb("vo_sb", [P, NP, C])
        latT = sb("latT", [P, NT * P], F32R)
        lat_all = sb("lat_all", [P, NT, 2, LAT], F32R)
        ones16 = sb("ones16", [P, P], BF16)
        pos = sb("pos", [P, NT], U32)
        tile_e = sb("tile_e", [1, NR], I32)

        w1_sb = sb("w1_sb", [C, E * FW])
        w2_sb = sb("w2_sb", [P, FB, E, C])
        b2_sb = sb("b2_sb", [3, E * C], BF16)

        rot_out = sb("rot_out", [P, 2, 2, 2 * S])
        staged = sb("staged", [P, 2, 2, 2, S])
        qk_sb = sb("qk_sb", [P, 2, NP, S])
        masked = sb("masked", [P, 2, SW])
        negmax = sb("negmax", [P, 2, 2])
        rowsum = sb("rowsum", [P, 4, 2])
        rden = sb("rden", [P, 4, 2])
        pexp = sb("pexp", [P, 4, SW])
        probs = sb("probs", [P, 2, SW])
        probsT = sb("probsT", [P, 2, 2, S], F32R)
        probsT_own = sb("probsT_own", [P, 2, P])
        lat = sb("lat", [P, 2, 3 * LAT], F32R)
        lat_own = sb("lat_own", [P, 3 * LAT])
        ctxT = sb("ctxT", [P, NP, S])
        y_keep = sb("y_keep", [P, 2, C])
        gated = sb("gated", [P, 2, C])
        res = sb("res", [P, 2, C])

        def start_tensors():
            with ExitStack() as ph:
                t = {}
                for name, shape, dt in (
                        ("wdnT", [C, 2 * LAT], F32),
                        ("wdnT_h", [C, 2 * LAT], F32R), ("wdnT_l", [C, 2 * LAT], F32R),
                        ("wv_sb", [P, NP, LAT], F32), ("wo_sb", [P, NP, C], F32),
                        ("gw", [C, E], F32), ("gw_h", [C, E], F32R), ("gw_l", [C, E], F32R), ("gb", [P, E], F32),
                        ("cex", [P, NT, E], F32), ("cexcl", [P, E, E], F32), ("cincl", [P, E, E], F32),
                        ("ctile", [1, NR, E], F32), ("cbef", [P, P], F32), ("cbef16", [P, P], BF16),
                        ("halfneg", [P, NT], F32), ("zeros", [P, C], F32),
                        ("st6", [P, NT, 6], F32), ("mv", [P, NT, 2], F32), ("veps", [P, NT], F32),
                        ("rstd", [P, NT], F32), ("lg", [P, NT, E], F32), ("top", [P, NT, E], F32),
                        ("topi", [P, NT, E], U32), ("topf", [P, NT, 2], F32), ("estar", [P, NT], F32),
                        ("hot", [P, NT, E], F32), ("hot16", [P, NT, E], BF16), ("cnt_i", [P, E], I32),
                        ("tiles_i", [P, E], I32), ("tiles_f", [P, E], F32), ("prod", [P, 2, E, E], F32),
                        ("base", [P, E], F32),
                        ("rank", [P, NT, E], F32), ("counts", [P, (NT + 1) * E], F32),
                        ("cmp", [1, NR, E], F32), ("tef", [1, NR], F32),
                        ("bias_in", [P, BW], F32), ("bias_rest", [P, 2, BW], F32), ("bias_parts", [P, 3, BW], BF16)):
                    t[name] = ph.enter_context(nc.sbuf_tensor(name, shape, dt))
                return t

        T = start_tensors()
        T["wq_in"] = w1_sb[:, 0:H * HD]
        T["wkup"] = w1_sb[:, H * HD:2 * H * HD]
        T["lgT"] = w1_sb[0:E, 2 * H * HD:2 * H * HD + NT * P]
        xsT = sb("xsT", [P, 2, P])
        w1_own = sb("w1_own", [P, 2, FW])
        hidT = sb("hidT", [P, 2, FB, P])
        xs = sb("xs", [P, 2, C])
        z = sb("z", [P, NR, C])

        NC_IN = 6

        x_in = [sem(f"x_in{q}") for q in range(4)]
        id_in = sem("id_in")
        c_in = sem("c_in")
        wk_in = sem("wk_in")
        wq_in = sem("wq_in")
        wd_in = sem("wd_in")
        w_in = sem("w_in")
        m_in = sem("m_in")
        f_in = sem("f_in")
        fb_in = sem("fb_in")
        fb_spread = sem("fb_spread")
        zero_ready = sem("zero_ready")
        zero_out = sem("zero_out")
        dve_step = sem("dve_step")
        var_ready = sem("var_ready")
        rstd_ready = sem("rstd_ready")
        xn_ready = sem("xn_ready")
        xT_done = sem("xT_done")
        xT_high = sem("xT_high")
        xT_low = sem("xT_low")
        wsplit_high = sem("wsplit_high")
        wsplit_low = sem("wsplit_low")
        wk_low = sem("wk_low")
        vo_done = sem("vo_done")
        vo_ready = sem("vo_ready")
        lg_done = sem("lg_done")
        lgT_done = sem("lgT_done")
        lgT_ready = sem("lgT_ready")
        latT_done = sem("latT_done")
        latT_high = sem("latT_high")
        latT_low = sem("latT_low")
        lat_turned = sem("lat_turned")
        lat_copied = sem("lat_copied")
        hot_ready = sem("hot_ready")
        cnt_done = sem("cnt_done")
        pos_ready = sem("pos_ready")
        tile_ready = sem("tile_ready")
        pool_step = sem("pool_step")
        cnt_read = sem("cnt_read")
        tiles_ready = sem("tiles_ready")
        bias_split = sem("bias_split")
        scattered = sem("scattered")

        proj_done = sem("proj_done")
        rope_done = sem("rope_done")
        staged_ready = sem("staged_ready")
        qk_in = [sem(f"qk_in{i}") for i in range(NG)]
        scores_done = sem("scores_done")
        masked_ready = sem("masked_ready")
        exp_done = sem("exp_done")
        rden_ready = sem("rden_ready")
        probs_ready = sem("probs_ready")
        probsT_done = sem("probsT_done")
        probsT_high = sem("probsT_high")
        probsT_ready = sem("probsT_ready")
        pv_done = sem("pv_done")
        ctx_ready = sem("ctx_ready")
        lat_ready = sem("lat_ready")
        y_done = sem("y_done")
        y_read = sem("y_read")
        res_ready = sem("res_ready")
        out_done = sem("out_done")
        scale_turn = sem("scale_turn")
        store_turn = sem("store_turn")

        xs_in = [sem(f"xs_in{i}") for i in range(2)]
        xsT_done = sem("xsT_done")
        xsT_ready = sem("xsT_ready")
        h_done = sem("h_done")
        hid_ready = sem("hid_ready")
        w1_ready = sem("w1_ready")
        e_done = sem("e_done")
        z_ready = sem("z_ready")
        g_ready = sem("g_ready")
        g_out = sem("g_out")
        g_in = sem("g_in")

        rows = (slice(0, P), slice(P, SW))

        def program(eng, start, body, finish, experts):
            start()
            body(0, False)
            finish(0)
            experts()
            body(1, False)
            with eng.Fori(2, B - 1) as b:
                body(b, False)
            body(B - 1, True)
            finish(B - 1)

        def over_tiles(eng, step):
            step(-1, 1)
            step(0, 0)
            step(1, 1)
            with eng.Fori(1, NR // 2 - 1) as m:
                step(2 * m, 0)
                step(2 * m + 1, 1)
            step(NR - 2, 0)
            step(NR - 1, 1)

        def experts_of(engine, first, count):
            return nc.values_load_multi_w_load_instructions(
                tile_e[0:1, bass.ds(first, count)], engines=[engine], min_val=0, max_val=E - 1)[1]

        def has(t, lead):
            return not isinstance(t, int) or 0 <= t + lead < NR

        def at(b, *which):
            return isinstance(b, int) and b in which

        def after(b, h):
            return (b, h + 1) if h + 1 < H else (b + 1, 0)

        def by_pool(b):
            return not at(b, 0, 1)

        block = ctx.enter_context(nc.Block())

        @block.sync
        def _(sp):
            def place(b, g):
                sp.wait_ge(staged_ready, NI * b + 2 * g + 2)
                sp.sem_inc(store_turn, 1)
                wait(sp, scores_done, H * b + HPG * (g + 1) - H)
                for hh in range(HPG):
                    for half in range(2):
                        to = HD * (hh % 2) + HALF * half
                        sp.dma_start(qk_sb[to:to + HALF, :, 2 * g + hh // 2, :],
                                     staged[HALF * hh:HALF * (hh + 1), g % 2, half]).then_inc(qk_in[g], 16)

            def start():
                sp.sem_inc(out_done, 16)
                xv = x.rearrange("b (n p) c -> p (b n) c", p=P)

                def rows_in(q):
                    n = slice(q * NT // 4, (q + 1) * NT // 4)
                    sp.dma_start(x_sb[:, n, :], xv[:, n, :]).then_inc(x_in[q], 16)
                rows_in(0)
                sp.dma_start(T["wdnT"][:], w_downT).then_inc(wd_in, 16)
                sp.dma_start(T["gw"][:], gate_w).then_inc(wd_in, 16)
                sp.dma_start(ident[:], c_ident).then_inc(id_in, 16)
                sp.dma_start(T["wq_in"][:], wqT).then_inc(wq_in, 16)
                sp.dma_start(T["wkup"][:], w_kupT).then_inc(wk_in, 16)
                rows_in(1)
                sp.dma_start(rot[:], c_rot).then_inc(m_in, 16)
                sp.dma_start(T["wv_sb"][:], w_vup).then_inc(w_in, 16)
                sp.dma_start(T["wo_sb"][:], woT).then_inc(w_in, 16)
                for q in range(2, 4):
                    rows_in(q)
                for dst, src in (("cex", c_expert), ("cexcl", c_excl), ("cincl", c_incl),
                                 ("cbef", c_before), ("ctile", c_tile[0:1]),
                                 ("gb", gate_b.rearrange("(a e) -> a e", a=1).broadcast_to([P, E]))):
                    sp.dma_start(T[dst][:], src).then_inc(c_in, 16)
                sp.dma_start(mask[:, 0:P], c_mask).then_inc(m_in, 16)
                sp.dma_start(mask[:, 2 * P:3 * P], c_mask).then_inc(m_in, 16)
                sp.dma_start(T["bias_in"][:], b2.rearrange("e (q f) -> (e q) f", f=BW)).then_inc(fb_in, 16)
                sp.wait_ge(zero_ready, 1)
                sp.dma_start(sorted_x.rearrange("(j p) c -> p j c", p=P),
                             T["zeros"][:].unsqueeze(1).broadcast_to([P, NR, C])).then_inc(zero_out, 16)
                for g in range(NG):
                    place(0, g)
                sp.wait_ge(wsplit_low, 3)
                sp.wait_ge(wk_low, 1)
                sp.wait_ge(lg_done, 1)
                w1_view = w1_sb[:].rearrange("p (e f) -> p e f", e=E)
                sp.dma_start(w1_view[:, :, 0:FF], w1.rearrange("e c f -> c e f")).then_inc(f_in, 16)
                sp.dma_start(w1_view[:, :, FF:FW], b1).then_inc(f_in, 16)
                for k in range(FB):
                    sp.dma_start(w2_sb[:, k], w2.rearrange("e (k p) c -> k p e c", p=P)[k]).then_inc(f_in, 16)
                sp.wait_ge(bias_split, 1)
                for i in range(3):
                    sp.dma_start(b2_sb[i:i + 1, :].rearrange("a (p f) -> a p f", p=P),
                                 T["bias_parts"][:, i, :]).then_inc(fb_spread, 16)

            def store(b):
                ov = out.rearrange("b (n p) c -> b p n c", p=P)[bass.ds(b, 1)].rearrange("a p n c -> (a p) n c")
                sp.dma_start(ov, res[:]).then_inc(out_done, 16)

            def body(b, last):
                if not at(b, 0):
                    place(b, NG - 1)
                if not at(b, 0, 1):
                    sp.wait_ge(res_ready, b - 1)
                    sp.sem_inc(store_turn, 1)
                    store(b - 1)
                if not last:
                    for g in range(NG - 1):
                        place(b + 1, g)
                else:
                    sp.wait_ge(res_ready, B - 1)
                    store(0)

            def finish(b):
                if b == B - 1:
                    sp.wait_ge(res_ready, B)
                    store(b)

            def experts():
                sp.wait_ge(scattered, 16 * NT)


                def load(t, i):
                    wait(sp, xsT_done, t - 1)
                    sp.dma_start(xs[:, i, :], sorted_x[bass.ds(t * P, P), :]).then_inc(xs_in[i], 16)
                load(0, 0)
                load(1, 1)
                with sp.Fori(1, NR // 2) as m:
                    for i in range(2):
                        load(2 * m + i, i)
                for q in range(2):
                    n = slice(q * NR // 2, (q + 1) * NR // 2)
                    sp.wait_ge(g_ready, q + 1)
                    sp.dma_start(sorted_g.rearrange("(j p) c -> p j c", p=P)[:, n, :], z[:, n, :]).then_inc(g_out, 16)

            program(sp, start, body, finish, experts)
            sp.wait_ge(out_done, 16 * B + 16)

        @block.gpsimd
        def _(pool):
            def rotated(b, n):
                pool.wait_ge(rope_done, NI * b + n + 1)
                g = n // 2
                if g >= 2:
                    pool.wait_ge(qk_in[g - 2], 128 * b + 128)
                else:
                    wait(pool, qk_in[g + 2], 128 * b)
                pool.tensor_tensor(staged[:, g % 2, :, n % 2, :], rot_out[:, n % 2, :, 0:S], rot_out[:, n % 2, :, S:2 * S],
                                   op=ALU.add).then_inc(staged_ready, 1)

            def scale(b, h):
                if at(b, 2):
                    pool.wait_ge(probs_ready, H * b)
                pool.wait_ge(rden_ready, H * b + h + 1)
                wait(pool, probsT_done, H * b + h - 1)
                pool.sem_inc(scale_turn, 1)
                for i, c in enumerate(rows):
                    m = pool.tensor_scalar(probs[:, h % 2, c], pexp[:, h % 4, c], rden[:, h % 4, i:i + 1], 1.0,
                                           ALU.mult, ALU.mult)
                m.then_inc(probs_ready, 1)

            step = [0]

            def then(ins):
                step[0] += 1
                ins.then_inc(pool_step, 1)
                pool.wait_ge(pool_step, step[0])

            def split_biases():
                parts, rest = T["bias_parts"], T["bias_rest"]
                pool.wait_ge(fb_in, 16)
                then(pool.tensor_copy(parts[:, 0, :], T["bias_in"][:]))
                then(pool.tensor_tensor(rest[:, 0, :], T["bias_in"][:], parts[:, 0, :], op=ALU.subtract))
                then(pool.tensor_copy(parts[:, 1, :], rest[:, 0, :]))
                then(pool.tensor_tensor(rest[:, 1, :], rest[:, 0, :], parts[:, 1, :], op=ALU.subtract))
                pool.tensor_copy(parts[:, 2, :], rest[:, 1, :]).then_inc(bias_split, 1)

            def add_up(v, width):
                half = width // 2
                while half >= 1:
                    o = v[..., 0:half]
                    ins = pool.tensor_tensor(o, v[..., 0:half], v[..., half:2 * half], op=ALU.add)
                    then(ins)
                    half //= 2

            def route_place():
                counts, prod, base, rank = T["counts"], T["prod"], T["base"], T["rank"]
                pool.wait_ge(cnt_read, 1)
                pool.wait_ge(tiles_ready, 1)
                tb = T["tiles_f"][:].unsqueeze(1).broadcast_to([P, E, E])
                pool.tensor_tensor(prod[:, 0], T["cexcl"][:], tb, op=ALU.mult)
                then(pool.tensor_tensor(prod[:, 1], T["cincl"][:], tb, op=ALU.mult))
                add_up(prod[:], E)
                then(pool.tensor_scalar(base[:], prod[:, 0, :, 0], float(P), None, ALU.mult))
                then(pool.tensor_tensor(rank[:], counts[:, 0:NT * E].rearrange("p (n e) -> p n e", e=E),
                                        base[:].unsqueeze(1).broadcast_to([P, NT, E]), op=ALU.add))
                then(pool.tensor_tensor(rank[:], rank[:], T["hot"][:], op=ALU.mult))
                add_up(rank[:], E)
                pool.tensor_copy(pos[:], rank[:, :, 0]).then_inc(pos_ready, 1)

            def scatter(n):
                if n == 0:
                    pool.wait_ge(zero_out, 16)
                    pool.wait_ge(pos_ready, 1)
                pool.indirect_dma_start(
                    out=sorted_x, out_offset=bass.IndirectOffsetOnAxis(ap=pos[:, n:n + 1], axis=0),
                    in_=xn[:, n, :], in_offset=None).then_inc(scattered, 16)

            def gather(n):
                if n == 0:
                    pool.wait_ge(scattered, 16 * NT)
                    pool.wait_ge(g_out, 32)
                pool.indirect_dma_start(
                    out=gate[:, n, :], out_offset=None, in_=sorted_g,
                    in_offset=bass.IndirectOffsetOnAxis(ap=pos[:, n:n + 1], axis=0)).then_inc(g_in, 16)

            def start():
                pool.memset(T["zeros"][:], 0.0).then_inc(zero_ready, 1)
                pool.memset(mask[:, P:2 * P], 0.0)
                pool.memset(lat[:].bitcast(F32), 0.0)
                pool.memset(lat_own[:], 0.0)
                pool.memset(T["halfneg"][:], -0.5).then_inc(zero_ready, 1)
                pool.wait_ge(zero_ready, 2)
                def rstd(q):
                    n = slice(q * NT // 4, (q + 1) * NT // 4)
                    pool.wait_ge(var_ready, q + 1)
                    pool.tensor_tensor(T["rstd"][:, n], T["veps"][:, n], T["halfneg"][:, n],
                                       op=ALU.pow).then_inc(rstd_ready, 1)
                rstd(0)
                pool.wait_ge(wsplit_high, 4)
                pool.tensor_tensor(wk_l[:], T["wkup"][:], wk_h[:].bitcast(F32), op=ALU.subtract).then_inc(wk_low, 1)
                rstd(1)
                for n in range(NI):
                    rotated(0, n)
                    if n in (0, 2):
                        rstd(n // 2 + 2)
                split_biases()

            def body(b, last):
                for h in range(H):
                    if at(b, 0) and h == 4:
                        route_place()
                    if not (last and h == H - 1) and by_pool(after(b, h)[0]):
                        scale(*after(b, h))
                    if h == 1 and not at(b, 0, 1):
                        rotated(b, NI - 1)
                    if h % 2 and h > 1 and not at(b, 0) and not last:
                        rotated(b + 1, (h - 3) // 2)
                    if at(b, 0, 1) and h >= 4:
                        for n in ((2 * h - 8, 2 * h - 7) if h < 8 else (h,)):
                            (scatter, gather)[b](n)

            program(pool, start, body, lambda b: None, lambda: None)

        @block.vector
        def _(dve):
            step = [0]

            def then(ins):
                step[0] += 1
                ins.then_inc(dve_step, 1)
                dve.wait_ge(dve_step, step[0])

            def rotate(b, n, r):
                if r == 0:
                    dve.wait_ge(proj_done, NI * b + n + 1)
                    wait(dve, staged_ready, NI * b + n - 1)
                m = dve.tensor_tensor(rot_out[:, n % 2, r, :], j_bank[n % 2][:], rot[:, r, :], op=ALU.mult)
                if r == 1:
                    m.then_inc(rope_done, 1)

            def rotated_second(n):
                g = n // 2
                dve.wait_ge(rope_done, NI + n + 1)
                dve.wait_ge(staged_ready, NI + n)
                if g >= 2:
                    dve.wait_ge(qk_in[g - 2], 256)
                else:
                    dve.wait_ge(qk_in[g + 2], 128)
                dve.tensor_tensor(staged[:, g % 2, :, n % 2, :], rot_out[:, n % 2, :, 0:S], rot_out[:, n % 2, :, S:2 * S],
                                  op=ALU.add).then_inc(staged_ready, 1)

            def row_max(b, h):
                for i, c in enumerate(rows):
                    t = dve.tensor_tensor_reduce(masked[:, h % 2, c], s_bank[h % 2][:, c], mask[:, c], -1.0, -NEG * 1e8,
                                                 ALU.add, ALU.min, negmax[:, h % 2, i:i + 1])
                t.then_inc(masked_ready, 1)

            def denominators(b, h, ahead=True):
                dve.wait_ge(exp_done, H * b + h + 1)
                if ahead:
                    dve.wait_ge(scores_done, H * b + h + 3)
                dve.reciprocal(rden[:, h % 4, :], rowsum[:, h % 4, :]).then_inc(rden_ready, 1)

            def scale(b, h):
                if h == 0:
                    dve.wait_ge(probs_ready, H)
                dve.wait_ge(rden_ready, H * b + h + 1)
                dve.wait_ge(probsT_done, H * b + h - 1)
                for i, c in enumerate(rows):
                    m = dve.tensor_scalar(probs[:, h % 2, c], pexp[:, h % 4, c], rden[:, h % 4, i:i + 1], None, ALU.mult)
                m.then_inc(probs_ready, 1)

            def probs_low(b, h):
                dve.wait_ge(probsT_high, H * b + h + 1)
                dve.tensor_tensor(probsT[:, h % 2, 1, :], t_bank[h % 2][:, 0:S], probsT[:, h % 2, 0, :].bitcast(F32),
                                  op=ALU.subtract).then_inc(probsT_ready, 1)

            def stats(q):
                dve.wait_ge(x_in[q], 16)
                n4 = range(q * NT // 4, (q + 1) * NT // 4)
                for n in n4:
                    last = dve.bn_stats(T["st6"][:, n, :], x_sb[:, n, :])
                then(last)
                for n in n4:
                    last = dve.bn_aggr(T["mv"][:, n, :], T["st6"][:, n, :])
                then(last)
                n = slice(q * NT // 4, (q + 1) * NT // 4)
                dve.tensor_scalar(T["veps"][:, n], T["mv"][:, n, 1], LN_EPS, None, ALU.add).then_inc(var_ready, 1)

            def normalise(q):
                dve.wait_ge(rstd_ready, q + 1)
                for n in range(q * NT // 4, (q + 1) * NT // 4):
                    dve.tensor_scalar(xn[:, n, :], x_sb[:, n, :], T["mv"][:, n, 0:1], T["rstd"][:, n:n + 1],
                                      ALU.subtract, ALU.mult).then_inc(xn_ready, 1)

            def turned_low(q):
                dve.wait_ge(xT_high, q + 1)
                c = slice(q * 512, (q + 1) * 512)
                dve.tensor_tensor(xnT_l[:, c], bank[q][:], xnT_h[:, c].bitcast(F32), op=ALU.subtract).then_inc(xT_low, 1)

            def route_top():
                top = T["top"]
                dve.wait_ge(lg_done, 1)
                then(dve.tensor_tensor(T["lg"][:], y_bank[:, 0:NT * E].rearrange("p (n e) -> p n e", e=E),
                                       T["gb"][:].unsqueeze(1).broadcast_to([P, NT, E]), op=ALU.add))
                for n in range(NT):
                    last = dve.max(top[:, n, :], T["lg"][:, n, :])
                then(last)

            def route_index():
                top, topi = T["top"], T["topi"]
                for n in range(NT):
                    last = dve.max_index(topi[:, n, :], top[:, n, :], T["lg"][:, n, :])
                then(last)
                then(dve.tensor_copy(T["topf"][:], topi[:, :, 0:2]))
                then(dve.tensor_reduce(T["estar"][:], T["topf"][:], X_AXIS, ALU.max))
                then(dve.tensor_tensor(T["hot"][:], T["cex"][:], T["estar"][:].unsqueeze(2).broadcast_to([P, NT, E]),
                                       op=ALU.is_equal))
                dve.tensor_copy(T["hot16"][:], T["hot"][:]).then_inc(hot_ready, 1)

            def count_tiles():
                dve.wait_ge(cnt_read, 1)
                then(dve.tensor_scalar(T["cnt_i"][:], T["counts"][:, NT * E:], float(P - 1), None, ALU.add))
                then(dve.tensor_scalar(T["tiles_i"][:], T["cnt_i"][:], 7, None, ALU.arith_shift_right))
                dve.tensor_copy(T["tiles_f"][:], T["tiles_i"][:]).then_inc(tiles_ready, 1)

            def tile_experts():
                dve.wait_ge(pos_ready, 1)
                then(dve.tensor_tensor(T["cmp"][:], T["prod"][0:1, 1, :, 0].unsqueeze(1).broadcast_to([1, NR, E]),
                                       T["ctile"][:], op=ALU.is_le))
                then(dve.tensor_reduce(T["tef"][:], T["cmp"][:], X_AXIS, ALU.add))
                dve.tensor_scalar(tile_e[:], T["tef"][:], float(E - 1), None, ALU.min).then_inc(tile_ready, 1)

            def start():
                def weight_low(n, lo, hi, whole, k):
                    dve.wait_ge(wsplit_high, n + 1)
                    dve.scalar_tensor_tensor(out=lo, in0=whole, scalar=k, in1=hi.bitcast(F32), op0=ALU.mult,
                                             op1=ALU.subtract).then_inc(wsplit_low, 1)

                def latents_low(q):
                    dve.wait_ge(latT_high, q + 1)
                    c = slice(q * 512, (q + 1) * 512)
                    dve.tensor_tensor(latT[LAT:P, c], bank[6][LAT:P, :], latT[LAT:P, c].bitcast(F32),
                                      op=ALU.subtract).then_inc(latT_low, 1)

                dve.memset(ones16[:], 1.0).then_inc(hot_ready, 1)
                stats(0)
                normalise(0)
                weight_low(0, T["wdnT_l"][:], T["wdnT_h"][:], T["wdnT"][:], 1.0)
                weight_low(1, T["gw_l"][:], T["gw_h"][:], T["gw"][:], 1.0)
                turned_low(0)
                stats(1)
                weight_low(2, wq_l[:], wq_h[:], T["wq_in"][:], HD ** -0.5)
                normalise(1)
                latents_low(0)
                dve.wait_ge(m_in, 48)
                for q in range(4):
                    for r in range(2):
                        rotate(0, 2 * q, r)
                    if q > 0:
                        latents_low(q)
                    if q < 2:
                        stats(q + 2)
                    if q < 3:
                        turned_low(q + 1)
                    for r in range(2):
                        rotate(0, 2 * q + 1, r)
                    if q < 2:
                        normalise(q + 2)
                dve.wait_ge(zero_ready, 2)
                for h in range(2):
                    dve.wait_ge(scores_done, h + 1)
                    row_max(0, h)
                dve.wait_ge(scores_done, 3)
                dve.wait_ge(exp_done, 1)
                row_max(0, 2)
                dve.wait_ge(c_in, 16 * NC_IN)
                dve.tensor_copy(T["cbef16"][:], T["cbef"][:]).then_inc(hot_ready, 1)
                denominators(0, 0, ahead=False)

            def latents(b):
                if at(b, 0):
                    dve.wait_ge(lat_copied, 1)
                wait(dve, pv_done, H * b)
                dve.tensor_copy(lat[:, :, LAT:2 * LAT],
                                lat_all[:, bass.ds(2 * b, 1), :, :].bitcast(F32).rearrange("p n s l -> p (n s) l"))
                own = lat_all[:, bass.ds(2 * b + 1, 1), :, :].bitcast(F32).rearrange("p n s l -> p (n s) l")
                dve.tensor_tensor(lat_own[:, LAT:2 * LAT], own[:, 0, :], own[:, 1, :], op=ALU.add).then_inc(lat_ready, 1)

            def gate_product(b):
                dve.wait_ge(y_done, b + 1)
                dve.wait_ge(g_in, 16 * NT)
                dve.wait_ge(out_done, 16 * b)
                dve.tensor_tensor(gated[:].rearrange("p n c -> p (n c)"), y_bank[:, 0:2 * C],
                                  gate[:, bass.ds(2 * b, 2), :].rearrange("p n c -> p (n c)"),
                                  op=ALU.mult).then_inc(y_read, 1)

            def residual(b):
                dve.wait_ge(y_read, b + 1)
                dve.tensor_tensor(res[:], gated[:], x_sb[:, bass.ds(2 * b, 2), :], op=ALU.add).then_inc(res_ready, 1)

            routing = {0: route_top, 1: route_index, 3: count_tiles, 8: tile_experts}

            def body(b, last):
                for h in range(H):
                    if not (last and h == H - 1):
                        denominators(*after(b, h), ahead=(h + 3 < H or not last))
                    if h + 3 < H:
                        row_max(b, h + 3)
                    elif not last:
                        row_max(b + 1, h + 3 - H)
                    if at(after(b, h)[0], 1):
                        scale(*after(b, h))
                    probs_low(b, h)
                    if h == 0:
                        latents(b)
                        if not at(b, 0, 1):
                            rotate(b, NI - 1, 1)
                    elif not last:
                        if h % 2:
                            rotate(b + 1, h // 2, 0)
                        else:
                            rotate(b + 1, h // 2 - 1, 1)
                            if at(b, 0):
                                rotated_second(h // 2 - 1)
                    if h == 2 and not at(b, 0, 1):
                        gate_product(b - 1)
                    if h == 3 and not at(b, 0, 1):
                        residual(b - 1)
                    if at(b, 0) and h in routing:
                        routing[h]()
                    if last and h == 8:
                        dve.wait_ge(out_done, 16 * (B - 1))
                        then(dve.tensor_tensor(y_keep[:], y_keep[:], gate[:, 0:2, :], op=ALU.mult))
                        dve.tensor_tensor(res[:], y_keep[:], x_sb[:, 0:2, :], op=ALU.add).then_inc(res_ready, 1)

            def finish(b):
                if b == 0:
                    rotate(1, NI - 1, 1)
                    rotated_second(NI - 1)
                    dve.wait_ge(y_done, 1)
                    dve.tensor_copy(y_keep[:].rearrange("p n c -> p (n c)"), y_bank[:, 0:2 * C]).then_inc(y_read, 1)
                else:
                    dve.wait_ge(out_done, 16 * B)
                    gate_product(b)
                    residual(b)

            def experts():
                def turned_rows(t, i):
                    dve.wait_ge(xsT_done, t + 1)
                    wait(dve, h_done, t - 1)
                    dve.tensor_copy(xsT[:, i, :], bank[i][:, 0:P]).then_inc(xsT_ready, 1)

                def step(t, i):
                    if has(t, 2):
                        turned_rows(t + 2, i)
                    if has(t, 0):
                        dve.wait_ge(e_done, t + 1)
                        dve.tensor_scalar(z[:, bass.ds(t, 1), :].rearrange("p a c -> p (a c)"), bank[6 + i][:, 0:C],
                                          float(TOP_K), None, ALU.mult).then_inc(z_ready, 1)
                turned_rows(0, 0)
                over_tiles(dve, step)

            program(dve, start, body, finish, experts)

        @block.scalar
        def _(act):
            def exponentials(b, h):
                act.wait_ge(masked_ready, H * b + h + 1)
                wait(act, probs_ready, H * b + h - 3)
                for i, c in enumerate(rows):
                    e = act.activation(pexp[:, h % 4, c], masked[:, h % 2, c], ACT.Exp, bias=negmax[:, h % 2, i:i + 1],
                                       scale=-1.0, accum_out=rowsum[:, h % 4, i:i + 1])
                e.then_inc(exp_done, 1)

            def scale(b, h):
                act.wait_ge(rden_ready, H * b + h + 1)
                wait(act, probsT_done, H * b + h - 1)
                for i, c in enumerate(rows):
                    m = act.mul(probs[:, h % 2, c], pexp[:, h % 4, c], rden[:, h % 4, i:i + 1])
                m.then_inc(probs_ready, 1)

            def probs_high(b, h):
                act.wait_ge(probsT_done, H * b + h + 1)
                wait(act, pv_done, H * b + h - 1)
                act.copy(probsT[:, h % 2, 0, :], t_bank[h % 2][:, 0:S])
                act.copy(probsT_own[:, h % 2, :], t_bank[h % 2][:, S:SW]).then_inc(probsT_high, 1)

            def read_counts():
                act.wait_ge(cnt_done, 1)
                act.copy(T["counts"][:], y_bank[:, 0:(NT + 1) * E]).then_inc(cnt_read, 1)

            def ctx_out(b, p):
                act.wait_ge(pv_done, H * b + 2 * p + 2)
                if p == 0:
                    wait(act, y_done, b)
                act.copy(ctxT[:, p, :], o_bank[:, 0:S]).then_inc(ctx_ready, 1)

            def start():
                act.wait_ge(wd_in, 32)
                act.copy(T["wdnT_h"][:], T["wdnT"][:]).then_inc(wsplit_high, 1)
                act.copy(T["gw_h"][:], T["gw"][:]).then_inc(wsplit_high, 1)

                def latents_copied(q):
                    act.wait_ge(lat_turned, q + 1)
                    act.copy(lat_all[:, q * NT // 4:(q + 1) * NT // 4].rearrange("p n s l -> p (n s l)"),
                             bank[7][:]).then_inc(lat_copied, 1)

                def turned(q):
                    act.wait_ge(xT_done, q + 1)
                    act.copy(xnT_h[:, q * 512:(q + 1) * 512], bank[q][:]).then_inc(xT_high, 1)

                turned(0)
                act.wait_ge(wq_in, 16)
                act.mul(wq_h[:], T["wq_in"][:], HD ** -0.5).then_inc(wsplit_high, 1)
                act.wait_ge(wk_in, 16)
                act.copy(wk_h[:], T["wkup"][:]).then_inc(wsplit_high, 1)
                for q in range(4):
                    c = slice(q * 512, (q + 1) * 512)
                    act.wait_ge(latT_done, q + 1)
                    act.copy(latT[:, c], bank[6][:]).then_inc(latT_high, 1)
                    act.wait_ge(lgT_done, q + 1)
                    act.copy(T["lgT"][:, c], bank[q][0:E, :]).then_inc(lgT_ready, 1)
                    if q < 3:
                        turned(q + 1)
                    if q == 0:
                        act.wait_ge(vo_done, 1)
                        for i in range(2):
                            act.copy(vo_sb[:, 4 * i:4 * i + 4, :].rearrange("p n c -> p (n c)"), bank[2 + i][:]).then_inc(vo_ready, 1)
                    elif q < 3:
                        latents_copied(q - 1)
                exponentials(0, 0)
                latents_copied(2)
                latents_copied(3)
                exponentials(0, 1)
                scale(0, 0)

            def body(b, last):
                for h in range(H):
                    if h + 2 < H:
                        exponentials(b, h + 2)
                    elif not last:
                        exponentials(b + 1, h + 2 - H)
                    probs_high(b, h)
                    if at(after(b, h)[0], 0):
                        scale(*after(b, h))
                    if h == 0 and not at(b, 0, 1):
                        ctx_out(b - 1, NP - 1)
                    if h % 2 == 0 and h > 0:
                        ctx_out(b, h // 2 - 1)
                    if at(b, 0) and h == 3:
                        read_counts()

            def finish(b):
                ctx_out(b, NP - 1)

            def experts():
                act.wait_ge(tile_ready, 1)
                act.wait_ge(f_in, 16 * (2 + FB))
                ids = list(experts_of(mybir.EngineType.Activation, 0, 2))

                def weights(t, i):
                    wait(act, h_done, t - 1)
                    wait(act, hid_ready, t - 1)
                    act.copy(w1_own[:, i, :], w1_sb[:, bass.ds(ids[i] * FW, FW)]).then_inc(w1_ready, 1)

                weights(0, 0)

                def step(t, i):
                    if has(t, 2):
                        if i == 0:
                            ids[:] = experts_of(mybir.EngineType.Activation, t + 2, 2)
                        weights(t + 2, i)
                    if has(t, 1):
                        wait(act, w1_ready, t + 2)
                        act.wait_ge(h_done, t + 2)
                        wait(act, e_done, t)
                        o = 1 - i
                        for k in range(FB):
                            a = act.activation(hidT[:, o, k, :], j_bank[o][:, k * P:(k + 1) * P], ACT.Gelu,
                                               bias=w1_own[:, o, FF + k:FF + k + 1])
                        a.then_inc(hid_ready, 1)
                over_tiles(act, step)
                for q in range(2):
                    n = slice(q * NR // 2, (q + 1) * NR // 2)
                    act.wait_ge(z_ready, (q + 1) * NR // 2)
                    act.activation(z[:, n, :], z[:, n, :], ACT.Silu).then_inc(g_ready, 1)

            program(act, start, body, finish, experts)

        @block.tensor
        def _(pe):
            def split_matmul(o, lhs, rhs, start=True, stop=True):
                (lh, ll), (rh, rl) = lhs, rhs
                pe.matmul(o, lh, rh, start=start, stop=False)
                pe.matmul(o, lh, rl, start=False, stop=False)
                return pe.matmul(o, ll, rh, start=False, stop=stop)

            def project(b, n):
                g = n // 2
                wait(pe, rope_done, NI * b + n - 1)
                for half in range(2):
                    c = slice((2 * g + half) * P, (2 * g + half + 1) * P)
                    o, t = j_bank[n % 2][:, half * S:(half + 1) * S], bass.ds(b * S, S)
                    if n % 2 == 0:
                        m = split_matmul(o, (wq_h[:, c], wq_l[:, c]), (xnT_h[:, t], xnT_l[:, t]))
                    else:
                        pe.matmul(o, wk_h[:, c], latT[:, t], start=True, stop=False)
                        m = pe.matmul(o, wk_l[:, c], latT[:, t], start=False, stop=True)
                m.then_inc(proj_done, 1)

            def scores(b, h):
                r, p = slice(HD * (h % 2), HD * (h % 2) + HD), h // 2
                if h % HPG == 0:
                    pe.wait_ge(qk_in[h // HPG], 128 * b + 128)
                wait(pe, masked_ready, H * b + h - 1)
                pe.matmul(s_bank[h % 2][:, 0:P], qk_sb[r, 0, p, 0:P], qk_sb[r, 1, p, 0:P], start=True, stop=True)
                pe.matmul(s_bank[h % 2][:, P:SW], qk_sb[r, 0, p, P:S], qk_sb[r, 1, p, :],
                          start=True, stop=True).then_inc(scores_done, 1)

            def turn(b, h):
                pe.wait_ge(probs_ready, H * b + h + 1)
                wait(pe, probsT_ready, H * b + h - 1)
                for k in range(3):
                    t = pe.transpose(t_bank[h % 2][:, k * P:(k + 1) * P], probs[:, h % 2, k * P:(k + 1) * P], ident[:])
                t.then_inc(probsT_done, 1)

            def values(b, h):
                if h == 0:
                    pe.wait_ge(lat_ready, b + 1)
                if h % 2 == 0:
                    wait(pe, ctx_ready, NP * b + h // 2)
                pe.wait_ge(probsT_ready, H * b + h + 1)
                c = slice(LAT, 3 * LAT) if h % 2 == 0 else slice(0, 2 * LAT)
                split_matmul(o_bank[:, 0:S], [lat[:, k, c] for k in range(2)],
                             [probsT[:, h % 2, k, :] for k in range(2)], start=(h % 2 == 0), stop=False)
                pe.matmul(o_bank[:, P:S], lat_own[:, c], probsT_own[:, h % 2, :], start=False,
                          stop=(h % 2 == 1)).then_inc(pv_done, 1)

            def output(b, p):
                if p == 0:
                    wait(pe, y_read, b)
                pe.wait_ge(ctx_ready, NP * b + p + 1)
                for i in range(2):
                    m = pe.matmul(y_bank[:, i * C:(i + 1) * C], ctxT[:, p, i * P:(i + 1) * P], vo_sb[:, p, :],
                                  start=(p == 0 and i == 0), stop=(p == NP - 1), skip_group_check=True)
                if p == NP - 1:
                    m.then_inc(y_done, 1)

            def turn_rows(q):
                for n in range(q * NT // 4, (q + 1) * NT // 4):
                    pe.wait_ge(xn_ready, n + 1)
                    t = pe.transpose(bank[q][:, (n % 4) * P:(n % 4 + 1) * P], xn[:, n, :], ident[:])
                t.then_inc(xT_done, 1)

            def count_tokens():
                hot16 = T["hot16"]
                pe.wait_ge(hot_ready, 3)
                pe.matmul(y_bank[:, 0:NT * E], T["cbef16"][:], hot16[:].rearrange("p n e -> p (n e)"),
                          start=True, stop=False, skip_group_check=True)
                for n in range(NT - 1):
                    pe.matmul(y_bank[:, (n + 1) * E:NT * E].rearrange("p (n e) -> p n e", e=E), ones16[:],
                              hot16[:, n:n + 1, :].broadcast_to([P, NT - 1 - n, E]),
                              start=False, stop=(n == NT - 2), skip_group_check=True)
                for n in range(NT):
                    m = pe.matmul(y_bank[:, NT * E:(NT + 1) * E], ones16[:], hot16[:, n, :], start=False, stop=(n == NT - 1),
                                  skip_group_check=True)
                m.then_inc(cnt_done, 1)

            def start():
                def latents_of(q):
                    c = slice(q * 512, (q + 1) * 512)
                    if q == 0:
                        pe.wait_ge(wsplit_low, 2)
                    pe.wait_ge(xT_low, q + 1)
                    wait(pe, latT_low, q)
                    split_matmul(bank[6][:], (T["wdnT_h"][:], T["wdnT_l"][:]), (xnT_h[:, c], xnT_l[:, c])).then_inc(latT_done, 1)
                    split_matmul(bank[q][0:E, :], (T["gw_h"][:], T["gw_l"][:]), (xnT_h[:, c], xnT_l[:, c])).then_inc(lgT_done, 1)

                def turn_latents(q):
                    pe.wait_ge(latT_low, q + 1)
                    wait(pe, lat_copied, q)
                    for n in range(4):
                        k = (4 * q + n) * P
                        m = pe.transpose(bank[7][:, n * P:(n + 1) * P], latT[:, k:k + P].bitcast(F32), ident[:])
                    m.then_inc(lat_turned, 1)

                pe.wait_ge(id_in, 16)
                turn_rows(0)
                for q in range(4):
                    latents_of(q)
                    if q == 0:
                        pe.wait_ge(wsplit_low, 3)
                    project(0, 2 * q)
                    if q == 1:
                        pe.wait_ge(vo_ready, 2)
                    if q < 3:
                        turn_rows(q + 1)
                    if q == 0:
                        pe.wait_ge(wk_low, 1)
                        pe.wait_ge(latT_low, 1)
                    project(0, 2 * q + 1)
                    if q == 0:
                        pe.wait_ge(w_in, 32)
                        for h in range(H):
                            r = slice(HD * (h % 2), HD * (h % 2) + HD)
                            m = pe.matmul(bank[2 + h // 8][r, (h // 2 % 4) * C:(h // 2 % 4 + 1) * C], T["wv_sb"][r, h // 2, :],
                                          T["wo_sb"][r, h // 2, :], start=True, stop=True)
                        m.then_inc(vo_done, 1)
                    elif q < 3:
                        turn_latents(q - 1)
                pe.wait_ge(lgT_ready, 2)
                for h in range(3):
                    scores(0, h)
                turn_latents(2)
                turn_latents(3)
                pe.wait_ge(lat_copied, 4)
                pe.wait_ge(lgT_ready, 4)
                for n in range(NT):
                    m = pe.transpose(y_bank[:, n * E:(n + 1) * E], T["lgT"][:, n * P:(n + 1) * P], ident[0:E, 0:E])
                m.then_inc(lg_done, 1)
            def body(b, last):
                for h in range(H):
                    if h + 3 < H:
                        scores(b, h + 3)
                    elif not last:
                        scores(b + 1, h + 3 - H)
                    turn(b, h)
                    if h > 0:
                        values(b, h - 1)
                    elif not at(b, 0, 1):
                        values(b - 1, H - 1)
                    if at(b, 0) and h == 2:
                        count_tokens()
                    if at(b, 0) and h == 7:
                        pe.wait_ge(cnt_read, 1)
                        for p in range(3):
                            output(b, p)
                    elif h == 1 and not at(b, 0, 1):
                        output(b - 1, NP - 1)
                    elif h % 2 and h >= (9 if at(b, 0) else 3):
                        output(b, h // 2 - 1)
                    if h % 2 == 0 and not last:
                        project(b + 1, h // 2)

            def finish(b):
                values(b, H - 1)
                output(b, NP - 1)

            def experts():
                pe.wait_ge(fb_spread, 48)
                pe.wait_ge(f_in, 16 * (2 + FB))
                pe.wait_ge(tile_ready, 1)
                pe.wait_ge(masked_ready, H + 3)
                pe.wait_ge(rope_done, 2 * NI)
                pe.wait_ge(y_read, 1)

                ids = [None] * 2

                def turn_tile(t, i):
                    pe.wait_ge(xs_in[i], (t - i) * 8 + 16)
                    wait(pe, xsT_ready, t - 1)
                    pe.transpose(bank[i][:, 0:P], xs[:, i, :], ident[:]).then_inc(xsT_done, 1)

                def step(t, i):
                    o = 1 - i
                    if has(t, 1):
                        pe.wait_ge(xsT_ready, t + 2)
                        pe.wait_ge(w1_ready, t + 2)
                        wait(pe, hid_ready, t)
                        for k in range(FB):
                            m = pe.matmul(j_bank[o][:, k * P:(k + 1) * P], w1_own[:, o, k * P:(k + 1) * P], xsT[:, o, :],
                                          start=True, stop=True)
                        m.then_inc(h_done, 1)
                    if has(t, 2):
                        turn_tile(t + 2, i)
                    if has(t, 0) and i == 0:
                        ids[:] = experts_of(mybir.EngineType.PE, t, 2)
                    if has(t, 0):
                        e = ids[i]
                        pe.wait_ge(hid_ready, t + 1)
                        wait(pe, z_ready, t - 1)
                        pe.matmul(bank[6 + i][:, 0:C], ones16[0:3, :], b2_sb[:, bass.ds(e * C, C)], start=True, stop=False)
                        for k in range(FB):
                            m = pe.matmul(bank[6 + i][:, 0:C], hidT[:, i, k, :],
                                          w2_sb[:, k, :, :].rearrange("p e c -> p (e c)")[:, bass.ds(e * C, C)],
                                          start=False, stop=(k == FB - 1))
                        m.then_inc(e_done, 1)
                turn_tile(0, 0)
                over_tiles(pe, step)
                pe.wait_ge(z_ready, NR)

            program(pe, start, body, finish, experts)


def kernel(**inputs):
    import concourse.bacc as bacc
    from concourse.bass_utils import run_bass_kernel_spmd

    g = {k: np.asarray(v) for k, v in inputs.items()}
    by_half = lambda w: w.reshape(NG, HPG, 2, HALF, -1).transpose(4, 0, 2, 1, 3).reshape(w.shape[1], H * HD)
    arrays = {
        "x": g["L0_attn_x"],
        "wqT": by_half(g["L0_attn_wq"]),
        "w_downT": np.tile(g["L0_attn_w_kv_down"].T, (1, 2)),
        "w_kupT": np.tile(by_half(g["L0_attn_w_k_up"]), (2, 1)),
        "w_vup": g["L0_attn_w_v_up"].reshape(NP, 2 * HD, LAT).transpose(1, 0, 2),
        "woT": g["L0_attn_wo"].reshape(C, NP, 2 * HD).transpose(2, 1, 0),
        "gate_w": g["L0_ffn_gate_w"],
        "gate_b": g["L0_ffn_gate_b"],
        "w1": g["L0_ffn_w1"],
        "b1": g["L0_ffn_b1"].reshape(E, FB, P).transpose(2, 0, 1),
        "w2": g["L0_ffn_w2"],
        "b2": g["L0_ffn_b2"],
        **host_constants(),
    }
    arrays = {k: np.ascontiguousarray(v) for k, v in arrays.items()}
    nc = bacc.Bacc("TRN2", target_bir_lowering=False, num_devices=1)
    aps = {k: nc.dram_tensor(f"in_{k}", v.shape, mybir.dt.from_np(v.dtype), kind="ExternalInput").ap()
           for k, v in arrays.items()}
    out = nc.dram_tensor("out", (B, S, C), F32, kind="ExternalOutput").ap()
    build(nc, **aps, out=out)
    r = run_bass_kernel_spmd(nc, [{f"in_{k}": v for k, v in arrays.items()}], core_ids=[0])
    return r.results[0]["out"]
```
